# Optimizing a Trainium2 kernel written in Bass

```python
import numpy as np
import jax
import jax.numpy as jnp

def _softmax(x, axis=-1):
    return jax.nn.softmax(x, axis=axis)

def _gelu(x):
    return jax.nn.gelu(x, approximate=True)

def _silu(x):
    return jax.nn.silu(x)

def _sigmoid(x):
    return jax.nn.sigmoid(x)

def _layernorm(x, axis=-1, eps=1e-05):
    m = jnp.mean(x, axis=axis, keepdims=True)
    v = jnp.var(x, axis=axis, keepdims=True)
    return (x - m) / jnp.sqrt(v + eps)

def _scatter_add(tgt, idx, src, axis=0):
    return tgt.at[idx].add(src)

def _segment_sum(src, seg, n):
    return jax.ops.segment_sum(src, seg, n)
kernel_name = 'mk_xattn_ffn_d2_seqx_r4_cdb3c2'

def setup_inputs(seed: int=0):
    np.random.seed(seed)
    _w = jnp.asarray

    def _rec_inputs():
        import jax
        import jax.numpy as jnp
        _rk = jax.random.key(seed)
        x = -0.000125 + 0.9999 * jax.random.normal(jax.random.fold_in(_rk, 1), (32, 128, 1024), jnp.float32)
        _lenS = 128 - jax.random.randint(jax.random.fold_in(_rk, 7), (32,), 0, max(1, 128 // 4) + 1, jnp.int32)
        _lenS2 = 128 - jax.random.randint(jax.random.fold_in(_rk, 8), (32,), 0, max(1, 128 // 4) + 1, jnp.int32)
        _ctx_4096P = jax.random.normal(jax.random.fold_in(_rk, 11), (32, 16, 1024), jnp.float32)
        _ctx_4096c = jax.random.dirichlet(jax.random.fold_in(_rk, 511), 0.3 * jnp.ones((16,), jnp.float32), (32, 128))
        _ctx_4096t = jnp.einsum('bsk,bkd->bsd', _ctx_4096c, _ctx_4096P)
        _ctx_4096t = _ctx_4096t * jax.lax.rsqrt(jnp.mean(jnp.square(_ctx_4096t)) + 1e-12) * 0.953939
        ctx_4096 = -1.52775e-05 + 0.999936 * (_ctx_4096t + 0.3 * jax.random.normal(jax.random.fold_in(_rk, 611), (32, 128, 1024), jnp.float32))
        return (x, ctx_4096)
    x, ctx_4096 = _rec_inputs()

    def _L0_xattn_setup():
        import jax, jax.numpy as jnp
        import numpy as np
        H = 8
        C = 2

        def _autocorrelation(Q, K, V):
            B, L, D = Q.shape
            d = D // H
            q = Q.reshape(B, L, H, d).transpose(0, 2, 1, 3)
            k = K.reshape(B, L, H, d).transpose(0, 2, 1, 3)
            v = V.reshape(B, L, H, d).transpose(0, 2, 1, 3)
            qf = jnp.fft.fft(q, axis=2)
            kf = jnp.fft.fft(k, axis=2)
            corr = jnp.fft.ifft(qf * jnp.conj(kf), axis=2).real
            topk = int(C * np.log(L))
            w, idx = jax.lax.top_k(corr.transpose(0, 1, 3, 2), topk)
            w = jax.nn.softmax(w, axis=-1)
            pos = jnp.arange(L)[:, None]
            out = jnp.zeros_like(v)
            for i in range(topk):
                g = jnp.minimum(idx[:, :, None, :, i] + pos, L - 1)
                out = out + w[:, :, None, :, i] * jnp.take_along_axis(v, g, axis=2)
            return out.transpose(0, 2, 1, 3).reshape(B, L, D)
        key = jax.random.key(seed)
        k1, k2, k3 = jax.random.split(key, 3)
        B, L, D = (16, 128, 1024)
        Q = jax.random.normal(k1, (B, L, D), dtype=jnp.float32)
        K = jax.random.normal(k2, (B, L, D), dtype=jnp.float32)
        V = jax.random.normal(k3, (B, L, D), dtype=jnp.float32)
        return {'Q': Q, 'K': K, 'V': V}
    _L0_xattn_all = _L0_xattn_setup()
    _L0_xattn_in = {k: v for k, v in _L0_xattn_all.items() if k in ()}
    del _L0_xattn_all

    def _L0_ffn_setup():
        import jax, jax.numpy as jnp
        import numpy as np
        D_IN = 1024
        D_OUT = 1024
        RANK = 16
        NUM_EXPERTS = 8
        TOP_K = 2
        SCALING = 32.0 / RANK
        key = jax.random.key(seed)
        ks = jax.random.split(key, 6)
        x = jax.random.normal(ks[0], (4, 512, D_IN), dtype=jnp.float32)
        W_base = jax.random.normal(ks[1], (D_OUT, D_IN), dtype=jnp.float32) * (1.0 / np.sqrt(D_IN))
        b_base = jax.random.normal(ks[2], (D_OUT,), dtype=jnp.float32) * 0.01
        W_router = jax.random.normal(ks[3], (NUM_EXPERTS, D_IN), dtype=jnp.float32) * 0.01
        A_stack = jax.random.uniform(ks[4], (NUM_EXPERTS, RANK, D_IN), dtype=jnp.float32, minval=-1.0, maxval=1.0) * (1.0 / np.sqrt(D_IN))
        B_stack = jax.random.normal(ks[5], (NUM_EXPERTS, D_OUT, RANK), dtype=jnp.float32) * 0.02
        return {'x': x, 'W_base': W_base, 'b_base': b_base, 'W_router': W_router, 'A_stack': A_stack, 'B_stack': B_stack}
    _L0_ffn_all = _L0_ffn_setup()
    _L0_ffn_in = {k: v for k, v in _L0_ffn_all.items() if k in ('W_base', 'b_base', 'W_router', 'A_stack', 'B_stack')}
    del _L0_ffn_all

    def _L1_xattn_setup():
        import jax, jax.numpy as jnp
        import numpy as np
        HEADS = 8
        WINDOW = 16

        def _pointwise(W, b, t):
            return jnp.einsum('oc,bct->bot', W, t) + b[None, :, None]
        key = jax.random.key(seed)
        ks = jax.random.split(key, 10)
        B, C, T = (4, 128, 1024)
        s = 0.02
        return {'x': jax.random.normal(ks[0], (B, C, T), jnp.float32), 'cond': jax.random.normal(ks[1], (B, C, T), jnp.float32), 'Wq': jax.random.normal(ks[2], (C, C), jnp.float32) * s, 'bq': jnp.zeros((C,), jnp.float32), 'Wk': jax.random.normal(ks[3], (C, C), jnp.float32) * s, 'bk': jnp.zeros((C,), jnp.float32), 'Wv': jax.random.normal(ks[4], (C, C), jnp.float32) * s, 'bv': jnp.zeros((C,), jnp.float32), 'Wo': jax.random.normal(ks[5], (C, C), jnp.float32) * s, 'bo': jnp.zeros((C,), jnp.float32)}
    _L1_xattn_all = _L1_xattn_setup()
    _L1_xattn_in = {k: v for k, v in _L1_xattn_all.items() if k in ('Wq', 'bq', 'Wk', 'bk', 'Wv', 'bv', 'Wo', 'bo')}
    del _L1_xattn_all

    def _L1_ffn_setup():
        import jax, jax.numpy as jnp
        import numpy as np
        LORA_R = 16
        SCALE = 16.0 / np.sqrt(16.0)
        NUM_EXPERTS = 4
        TOP_K = 2
        IN_F = 1024
        OUT_F = 1024
        key = jax.random.key(seed)
        k_x, k_a, k_b, k_r = jax.random.split(key, 4)
        x = jax.random.normal(k_x, (2, 512, IN_F), dtype=jnp.float32)
        A = jax.random.normal(k_a, (NUM_EXPERTS, LORA_R, IN_F), dtype=jnp.float32) * (1.0 / np.sqrt(IN_F))
        B = jax.random.normal(k_b, (NUM_EXPERTS, OUT_F, LORA_R), dtype=jnp.float32) * 0.02
        Wr = jax.random.normal(k_r, (NUM_EXPERTS, IN_F), dtype=jnp.float32) * 0.02
        return {'x': x, 'A': A, 'B': B, 'Wr': Wr}
    _L1_ffn_all = _L1_ffn_setup()
    _L1_ffn_in = {k: v for k, v in _L1_ffn_all.items() if k in ('A', 'B', 'Wr')}
    del _L1_ffn_all
    return {'x': x, 'ctx_4096': ctx_4096, 'L0_ffn_W_base': _L0_ffn_in['W_base'], 'L0_ffn_b_base': _L0_ffn_in['b_base'], 'L0_ffn_W_router': _L0_ffn_in['W_router'], 'L0_ffn_A_stack': _L0_ffn_in['A_stack'], 'L0_ffn_B_stack': _L0_ffn_in['B_stack'], 'L1_xattn_Wq': _L1_xattn_in['Wq'], 'L1_xattn_bq': _L1_xattn_in['bq'], 'L1_xattn_Wk': _L1_xattn_in['Wk'], 'L1_xattn_bk': _L1_xattn_in['bk'], 'L1_xattn_Wv': _L1_xattn_in['Wv'], 'L1_xattn_bv': _L1_xattn_in['bv'], 'L1_xattn_Wo': _L1_xattn_in['Wo'], 'L1_xattn_bo': _L1_xattn_in['bo'], 'L1_ffn_A': _L1_ffn_in['A'], 'L1_ffn_B': _L1_ffn_in['B'], 'L1_ffn_Wr': _L1_ffn_in['Wr']}

def reference(x, ctx_4096, L0_ffn_W_base, L0_ffn_b_base, L0_ffn_W_router, L0_ffn_A_stack, L0_ffn_B_stack, L1_xattn_Wq, L1_xattn_bq, L1_xattn_Wk, L1_xattn_bk, L1_xattn_Wv, L1_xattn_bv, L1_xattn_Wo, L1_xattn_bo, L1_ffn_A, L1_ffn_B, L1_ffn_Wr):
    import jax
    import jax.numpy as jnp

    def _L0_xattn_ref(Q, K, V):
        import jax, jax.numpy as jnp
        import numpy as np
        H = 8
        C = 2

        def _autocorrelation(Q, K, V):
            B, L, D = Q.shape
            d = D // H
            q = Q.reshape(B, L, H, d).transpose(0, 2, 1, 3)
            k = K.reshape(B, L, H, d).transpose(0, 2, 1, 3)
            v = V.reshape(B, L, H, d).transpose(0, 2, 1, 3)
            qf = jnp.fft.fft(q, axis=2)
            kf = jnp.fft.fft(k, axis=2)
            corr = jnp.fft.ifft(qf * jnp.conj(kf), axis=2).real
            topk = int(C * np.log(L))
            w, idx = jax.lax.top_k(corr.transpose(0, 1, 3, 2), topk)
            w = jax.nn.softmax(w, axis=-1)
            pos = jnp.arange(L)[:, None]
            out = jnp.zeros_like(v)
            for i in range(topk):
                g = jnp.minimum(idx[:, :, None, :, i] + pos, L - 1)
                out = out + w[:, :, None, :, i] * jnp.take_along_axis(v, g, axis=2)
            return out.transpose(0, 2, 1, 3).reshape(B, L, D)
        return _autocorrelation(Q, K, V)

    def _L0_ffn_ref(x, W_base, b_base, W_router, A_stack, B_stack):
        import jax, jax.numpy as jnp
        import numpy as np
        D_IN = 1024
        D_OUT = 1024
        RANK = 16
        NUM_EXPERTS = 8
        TOP_K = 2
        SCALING = 32.0 / RANK
        orig_shape = x.shape
        xf = x.reshape(-1, D_IN)
        logits = xf @ W_router.T
        probs = jax.nn.softmax(logits, axis=-1)
        topk_p, topk_i = jax.lax.top_k(probs, TOP_K)
        topk_p = topk_p / jnp.sum(topk_p, axis=-1, keepdims=True)
        combine = jnp.sum(jax.nn.one_hot(topk_i, NUM_EXPERTS, dtype=xf.dtype) * topk_p[..., None], axis=1)
        h = jnp.einsum('nd,erd->ner', xf, A_stack)
        h = h * combine[..., None]
        lora_out = jnp.einsum('ner,eor->no', h, B_stack) * SCALING
        base_out = xf @ W_base.T + b_base
        out = base_out + lora_out
        return out.reshape(orig_shape[:-1] + (D_OUT,))

    def _L1_xattn_ref(x, cond, Wq, bq, Wk, bk, Wv, bv, Wo, bo):
        import jax, jax.numpy as jnp
        import numpy as np
        HEADS = 8
        WINDOW = 16

        def _pointwise(W, b, t):
            return jnp.einsum('oc,bct->bot', W, t) + b[None, :, None]
        B, C, T = x.shape
        H, W = (HEADS, WINDOW)
        hd = C // H
        scale = hd ** (-0.5)
        pad_left = W // 2
        pad_right = W - pad_left - 1
        q = _pointwise(Wq, bq, x)
        k = _pointwise(Wk, bk, cond)
        v = _pointwise(Wv, bv, cond)
        k = jnp.pad(k, ((0, 0), (0, 0), (pad_left, pad_right)))
        v = jnp.pad(v, ((0, 0), (0, 0), (pad_left, pad_right)))
        idx = jnp.arange(T)[:, None] + jnp.arange(W)[None, :]
        k_win = k[:, :, idx].reshape(B, H, hd, T, W)
        v_win = v[:, :, idx].reshape(B, H, hd, T, W)
        qh = q.reshape(B, H, hd, T)
        dots = jnp.einsum('bhdt,bhdtw->bhtw', qh, k_win) * scale
        attn = jax.nn.softmax(dots, axis=-1)
        out = jnp.einsum('bhtw,bhdtw->bhdt', attn, v_win)
        out = out.reshape(B, C, T)
        return _pointwise(Wo, bo, out)

    def _L1_ffn_ref(x, A, B, Wr):
        import jax, jax.numpy as jnp
        import numpy as np
        LORA_R = 16
        SCALE = 16.0 / np.sqrt(16.0)
        NUM_EXPERTS = 4
        TOP_K = 2
        IN_F = 1024
        OUT_F = 1024
        orig_shape = x.shape
        flat = x.reshape(-1, orig_shape[-1])
        logits = flat @ Wr.T
        topk_vals, topk_idx = jax.lax.top_k(logits, TOP_K)
        T = flat.shape[0]
        neg_inf = jnp.finfo(logits.dtype).min
        sparse = jnp.full_like(logits, neg_inf)
        rows = jnp.arange(T)[:, None]
        sparse = sparse.at[rows, topk_idx].set(topk_vals)
        gates = jax.nn.softmax(sparse, axis=-1)
        mid = jnp.einsum('tf,erf->ter', flat, A)
        all_deltas = jnp.einsum('ter,eor->teo', mid, B) * SCALE
        delta = jnp.sum(gates[:, :, None] * all_deltas, axis=1)
        return delta.reshape(*orig_shape[:-1], -1)
    x = x + _L0_xattn_ref(_layernorm(x, axis=-1), ctx_4096, ctx_4096)
    x = x + _L0_ffn_ref(_layernorm(x, axis=-1), L0_ffn_W_base, L0_ffn_b_base, L0_ffn_W_router, L0_ffn_A_stack, L0_ffn_B_stack)
    x = x + _L1_xattn_ref(_layernorm(x, axis=-1), ctx_4096, L1_xattn_Wq, L1_xattn_bq, L1_xattn_Wk, L1_xattn_bk, L1_xattn_Wv, L1_xattn_bv, L1_xattn_Wo, L1_xattn_bo)
    x = x + _L1_ffn_ref(_layernorm(x, axis=-1), L1_ffn_A, L1_ffn_B, L1_ffn_Wr)
    return x

_drawn_inputs = setup_inputs


def setup_inputs(seed=0):
    import zlib

    import numpy as np

    out = dict(_drawn_inputs(seed))
    spreads = {'L1_xattn_bq': (0.0, 0.8),
     'L1_xattn_bk': (0.0, 0.8),
     'L1_xattn_bv': (0.0, 0.608),
     'L1_xattn_bo': (0.0, 0.1)}
    factors = {'L0_ffn_b_base': 6.527,
     'L1_xattn_Wq': 8.0,
     'L1_xattn_Wk': 8.0,
     'L1_xattn_Wv': 5.632,
     'L1_xattn_Wo': 3.611}
    for name, (base, spread) in spreads.items():
        noise = np.random.default_rng([zlib.crc32(name.encode()), seed]).standard_normal(out[name].shape)
        drawn = base * np.exp(spread * noise) if base else spread * noise
        out[name] = jnp.asarray(drawn.astype(out[name].dtype))
    for name, factor in factors.items():
        out[name] = (out[name] * factor).astype(out[name].dtype)
    return out
```

```python
import math
from contextlib import ExitStack

import numpy as np

import concourse.bass as bass
from concourse import mybir

F32 = mybir.dt.float32
I32 = mybir.dt.int32
ALU = mybir.AluOpType
ACT = mybir.ActivationFunctionType
AX_X = mybir.AxisListType.X

P = 128
GONE = -3.0e38
GONE_MAX = -2.9e38
TAKEN = 3.0e38
TAKEN_MIN = 2.9e38
RSQRT_MAGIC = 0x5F3759DF
RSQRT_NEWTON = 3
RSQRT_STEPS = 2 + 4 * RSQRT_NEWTON


class Signal:

    def __init__(self, sem, per):
        self.sem = sem
        self.per = per

    def after(self, b, k=None):
        return b * self.per + (self.per if k is None else k)


def spectral_tables():
    n = P
    half = n // 2
    t = np.arange(n, dtype=np.float64)
    k = np.arange(half, dtype=np.float64)
    even = 2.0 * np.pi * np.outer(t, k) / n
    odd = 2.0 * np.pi * np.outer(t, k + 0.5) / n
    alt = (-1.0) ** t

    fwd_a = np.concatenate([np.cos(even), -np.sin(even)], 1)
    fwd_a[:, half] = alt
    fwd_b = np.concatenate([np.cos(even), np.cos(even)], 1)
    fwd_b[:, half] = alt
    fwd_c = np.concatenate([-np.sin(even), -np.sin(even)], 1)
    fwd_c[:, 0] = 0.0
    fwd_c[:, half] = 0.0
    odd_a = np.concatenate([np.cos(odd), -np.sin(odd)], 1)
    odd_b = np.concatenate([np.cos(odd), np.cos(odd)], 1)
    odd_c = np.concatenate([-np.sin(odd), -np.sin(odd)], 1)

    def minus_last(f):
        f = f.copy()
        f[n - 1] -= f.sum(0)
        return f

    fwd_b, fwd_c, odd_b, odd_c = map(minus_last, (fwd_b, fwd_c, odd_b, odd_c))
    fwd_c[n - 1, 0] = 1.0

    scale = np.full((half, 1), 2.0 / n)
    scale[0] = 1.0 / n
    cos_e, sin_e = scale * np.cos(even).T, scale * np.sin(even).T
    corr_1 = np.concatenate([cos_e, -sin_e])
    corr_2 = np.concatenate([sin_e, cos_e])
    corr_1[half] = alt / n
    corr_2[0] = 0.0
    corr_2[half] = 0.0
    agg_1 = np.concatenate([cos_e, sin_e]) / 2
    agg_2 = np.concatenate([-sin_e, cos_e]) / 2
    agg_1[half] = alt / n / 2
    agg_2[0] = 1.0
    agg_2[half] = 0.0
    cos_o, sin_o = np.cos(odd).T * (1.0 / n), np.sin(odd).T * (1.0 / n)
    agg_3 = np.concatenate([cos_o, sin_o])
    agg_4 = np.concatenate([-sin_o, cos_o])
    tables = [fwd_a, fwd_b, fwd_c, odd_a, odd_b, odd_c, corr_1, corr_2, agg_1, agg_2, agg_3, agg_4]
    return np.stack([m.astype(np.float32) for m in tables], 1)


(FWD_A, FWD_B, FWD_C, ODD_A, ODD_B, ODD_C, CORR_1, CORR_2, AGG_1, AGG_2, AGG_3, AGG_4) = range(12)


def build(nc, x, ctx_in, spectra, identity, band, parity, base_w, base_b, ra0, b0, wqkvo, biases,
          ra1, b1, out):
    BATCH, _, D = x.shape
    KT = D // P
    HALF = D // 2
    E0, E1 = 8, 4
    RANK = 16
    SCALE0, SCALE1 = 32.0 / RANK, 16.0 / math.sqrt(16.0)
    HEADS, WINDOW = 8, 16
    HD = P // HEADS
    QB = 16
    NBLK = D // QB
    KEYS = 2 * QB
    PAD = WINDOW // 2
    NG = 4
    GB = NBLK // NG
    ATT_SCALE = HD ** -0.5
    TOPK = int(2 * np.log(P))
    assert TOPK == 9 and D == 1024

    ctx = ExitStack()
    with ctx:
        def sb(name, shape, dt=F32):
            return ctx.enter_context(nc.sbuf_tensor(name, shape, dt))

        def signal(name, per=1):
            return Signal(ctx.enter_context(nc.semaphore(name)), per)

        tab = sb("tab", [P, 12, P])
        ident = sb("ident", [P, P])
        band_mask = sb("band_mask", [P, KEYS])
        par = sb("par", [P, 2])
        w_base = sb("w_base", [P, KT, D])
        bias_base = sb("bias_base", [P, D])
        w_ra0 = sb("w_ra0", [P, KT, E0 + P])
        w_b0 = sb("w_b0", [P, D])
        w_att = sb("w_att", [P, 4, P])
        bias_att = sb("bias_att", [P, 4])
        bias_q = sb("bias_q", [P, 2])
        w_ra1 = sb("w_ra1", [P, KT, E1 + E1 * RANK])
        w_b1 = sb("w_b1", [E1 * RANK, D])

        x_a = sb("x_a", [P, D])
        ctx_a = sb("ctx_a", [P, D])
        xn_a = sb("xn_a", [P, D])
        wt = xn_a
        q_spec = sb("q_spec", [P, D])
        w_odd = q_spec
        v_b = sb("v_b", [P, D])
        v_c = sb("v_c", [P, D])
        p1 = sb("p1", [P, D])
        p2 = sb("p2", [P, D])
        rest = sb("rest", [P, KT, P])
        p3 = rest[:, :, :].rearrange("p a b -> p (a b)")
        prob = sb("prob", [P, KT, P])
        p4 = prob[:, :, :].rearrange("p a b -> p (a b)")
        top8 = sb("top8", [P, KT, 8])
        ninth = sb("ninth", [P, KT, 8])
        neg_max = sb("neg_max", [P, KT])
        psum_w = sb("psum_w", [P, KT])
        rec_w = sb("rec_w", [P, KT])

        x_r = sb("x_r", [P, D])
        ctx_r = sb("ctx_r", [P, D])
        xn_r = sb("xn_r", [P, D])
        xt = sb("xt", [P, D])
        lg = [sb(f"lg{n}", [P, 16]) for n in range(2)]
        lg_top = sb("lg_top", [P, 8])
        lg_pick = sb("lg_pick", [P, 8])
        lg_mark = sb("lg_mark", [P, 16])
        lg_neg = sb("lg_neg", [P, 1])
        lg_exp = sb("lg_exp", [P, E0])
        gate = sb("gate", [P, E0])
        gate_sum = sb("gate_sum", [P, 1])
        gate_rec = sb("gate_rec", [P, 1])
        mid = sb("mid", [P, P])
        mid_t = sb("mid_t", [P, P])
        q_diag = sb("q_diag", [P, NBLK, P])
        k_pad = sb("k_pad", [P, D + 2 * PAD])
        v_pad = sb("v_pad", [P, D + 2 * PAD])
        v_t = sb("v_t", [P, 2, NBLK // 2, KEYS])
        v_diag = sb("v_diag", [P, NBLK, 2, P // 2])
        sc = sb("sc", [P, NBLK, KEYS])
        sc_t = v_t[:, :, :, :].rearrange("p o m k -> p (o m) k")
        sc_max = sb("sc_max", [P, NBLK])
        sc_sum = sb("sc_sum", [P, NBLK])
        sc_rec = sb("sc_rec", [P, NBLK])

        bn = [sb(f"bn{n}", [P, 2, 6]) for n in range(4)]
        mv = [sb(f"mv{n}", [P, 2]) for n in range(4)]
        rs_v = [sb(f"rs_v{n}", [P, 1]) for n in range(4)]
        rs_t = [sb(f"rs_t{n}", [P, 1]) for n in range(4)]
        rs_y = [sb(f"rs_y{n}", [P, 1]) for n in range(4)]

        pa = ctx.enter_context(nc.psum_tensor("pa", [P, 4, HALF], F32))
        pr = ctx.enter_context(nc.psum_tensor("pr", [P, 4, HALF], F32))
        pa_lo = pa[:, 0:2, :].rearrange("p a b -> p (a b)")
        pa_hi = pa[:, 2:4, :].rearrange("p a b -> p (a b)")
        pr_lo = pr[:, 0:2, :].rearrange("p a b -> p (a b)")
        pr_hi = pr[:, 2:4, :].rearrange("p a b -> p (a b)")

        const_in = signal("const_in")
        const_set = signal("const_set")
        CONSTS_SET = 9
        x_in = signal("x_in", 16)
        ctxa_in = signal("ctxa_in", 16)
        ctxr_in = signal("ctxr_in", 16)
        out_done = signal("out_done", 16)
        ln_bn = [signal(f"ln_bn{n}", 2) for n in range(4)]
        ln_mv = [signal(f"ln_mv{n}") for n in range(4)]
        ln_rs = [signal(f"ln_rs{n}", RSQRT_STEPS) for n in range(4)]
        ln_out = [signal(f"ln_out{n}") for n in range(4)]
        mm_vb = signal("mm_vb")
        mm_vc = signal("mm_vc")
        mm_q = signal("mm_q")
        vb_out = signal("vb_out")
        vc_out = signal("vc_out")
        q_out = signal("q_out")
        prod_q = signal("prod_q", 2)
        mm_corr = signal("mm_corr", 2)
        top_found = signal("top_found", KT)
        top_gone = signal("top_gone", KT)
        negmax_out = signal("negmax_out", 2)
        ninth_found = signal("ninth_found")
        ninth_gone = signal("ninth_gone", KT)
        exp_out = signal("exp_out", KT)
        prob_masked = signal("prob_masked", KT)
        rec_out = signal("rec_out")
        prob_out = signal("prob_out")
        tr_w = signal("tr_w", 2)
        wt_out = signal("wt_out", 2)
        mm_we = signal("mm_we")
        mm_wo = signal("mm_wo")
        wo_out = signal("wo_out")
        prod_e = signal("prod_e", 2)
        mm_bo = signal("mm_bo")
        mm_co = signal("mm_co")
        prod_o = signal("prod_o", 2)
        mm_agg = signal("mm_agg")
        x1_out = signal("x1_out")
        tr_x = [signal(f"tr_x{n}", 2) for n in range(2)]
        xt_out = [signal(f"xt_out{n}", 2) for n in range(2)]
        mm_ra = [signal(f"mm_ra{n}") for n in range(2)]
        gt = [signal(f"gt{n}", 8) for n in range(2)]
        gt_exp = [signal(f"gt_exp{n}") for n in range(2)]
        mid_out = [signal(f"mid_out{n}") for n in range(2)]
        tr_mid = [signal(f"tr_mid{n}") for n in range(2)]
        midt_out = [signal(f"midt_out{n}") for n in range(2)]
        bias_added = signal("bias_added")
        mm_ffn = [signal(f"mm_ffn{n}") for n in range(2)]
        x2_out = signal("x2_out")
        x4_out = signal("x4_out")
        mm_k = signal("mm_k")
        mm_v = signal("mm_v")
        mm_qq = signal("mm_qq")
        k_out = signal("k_out")
        v_out = signal("v_out")
        qd_out = signal("qd_out", HEADS)
        vt_out = signal("vt_out", 2)
        vd_out = signal("vd_out", 8)
        mm_sc = signal("mm_sc", NG)
        sc_in = signal("sc_in", NG)
        sc_less = signal("sc_less", 2 * NG)
        sc_norm = signal("sc_norm", 3 * NG)
        sc_exp = signal("sc_exp", NG)
        sct_out = signal("sct_out", NG)
        mm_av = signal("mm_av", NG)
        av_out = signal("av_out", 2)
        mm_o = signal("mm_o")
        x3_out = signal("x3_out")

        idle_dve = sb("idle_dve", [P, 1])
        idle_pool = sb("idle_pool", [P, 1])

        def dve_wait(dve, signal, value):
            dve.wait_ge(signal.sem, value)
            nc.vector.memset(idle_dve[:, :], 0.0)

        def pool_wait(pool, signal, value):
            pool.wait_ge(signal.sem, value)
            nc.gpsimd.tensor_tensor(idle_pool[:, :], ident[:, 0:1], ident[:, 0:1], ALU.add)

        block = ctx.enter_context(nc.Block())

        consts = [(tab, spectra), (ident, identity), (band_mask, band), (par, parity),
                  (w_ra0, ra0), (w_base, base_w), (w_b0, b0), (w_att, wqkvo), (bias_att, biases),
                  (w_ra1, ra1), (w_b1, b1)]
        CONSTS_IN = 16 * (len(consts) + 1)

        @block.sync
        def _(sp):
            def load_x(b):
                sp.dma_start(x_a[:, :], x[b]).then_inc(x_in.sem, 16)

            def load_ctx_a(b):
                sp.dma_start(ctx_a[:, :], ctx_in[b]).then_inc(ctxa_in.sem, 16)

            def load_ctx_r(b):
                sp.dma_start(ctx_r[:, :], ctx_in[b]).then_inc(ctxr_in.sem, 16)

            def store(b):
                sp.wait_ge(x4_out.sem, x4_out.after(b))
                sp.dma_start(out[b], xn_r[:, :]).then_inc(out_done.sem, 16)

            load_x(0)
            load_ctx_a(0)
            for place, source in consts:
                sp.dma_start(place[:], source).then_inc(const_in.sem, 16)
            sp.dma_start(bias_base[:, :], base_b.partition_broadcast(P)).then_inc(const_in.sem, 16)
            load_ctx_r(0)
            sp.wait_ge(mm_co.sem, mm_co.after(0))
            load_ctx_a(1)
            sp.wait_ge(x1_out.sem, x1_out.after(0))
            load_x(1)

            with sp.Fori(1, BATCH - 1) as b:
                sp.wait_ge(mm_v.sem, mm_v.after(b - 1))
                load_ctx_r(b)
                sp.wait_ge(mm_co.sem, mm_co.after(b))
                load_ctx_a(b + 1)
                sp.wait_ge(x1_out.sem, x1_out.after(b))
                load_x(b + 1)
                store(b - 1)
            sp.wait_ge(mm_v.sem, mm_v.after(BATCH - 2))
            load_ctx_r(BATCH - 1)
            store(BATCH - 2)
            store(BATCH - 1)
            sp.wait_ge(out_done.sem, out_done.after(BATCH - 1))

        @block.tensor
        def _(pe):
            mm = nc.tensor.matmul

            def project(place, n, moving, lhsT):
                for h in range(2):
                    last = mm(place[:, n + h, :], lhsT, moving[:, h * HALF:(h + 1) * HALF],
                              start=True, stop=True)
                return last

            def a_context(b):
                pe.wait_ge(ctxa_in.sem, ctxa_in.after(b))
                if not (isinstance(b, int) and b == 0):
                    pe.wait_ge(prod_o.sem, prod_o.after(b - 1))
                project(pa, 0, ctx_a, tab[:, FWD_B, :]).then_inc(mm_vb.sem, 1)
                if not (isinstance(b, int) and b == 0):
                    pe.wait_ge(x1_out.sem, x1_out.after(b - 1))
                project(pa, 2, ctx_a, tab[:, FWD_C, :]).then_inc(mm_vc.sem, 1)

            def a_query(b):
                pe.wait_ge(vb_out.sem, vb_out.after(b))
                pe.wait_ge(ln_out[0].sem, ln_out[0].after(b))
                project(pa, 0, xn_a, tab[:, FWD_A, :]).then_inc(mm_q.sem, 1)

            def a_corr(b):
                pe.wait_ge(prod_q.sem, prod_q.after(b))
                pe.wait_ge(q_out.sem, q_out.after(b))
                for j in range(KT):
                    place = pa[:, j // 4, (j % 4) * P:(j % 4 + 1) * P]
                    mm(place, p1[:, j * P:(j + 1) * P], tab[:, CORR_1, :], start=True, stop=False)
                    last = mm(place, p2[:, j * P:(j + 1) * P], tab[:, CORR_2, :], start=False, stop=True)
                    if j % 4 == 3:
                        last.then_inc(mm_corr.sem, 1)

            def a_weights(b):
                pe.wait_ge(prob_out.sem, prob_out.after(b))
                pe.wait_ge(vc_out.sem, vc_out.after(b))
                for j in range(KT):
                    place = pa[:, 2 + j // 4, (j % 4) * P:(j % 4 + 1) * P]
                    last = nc.tensor.transpose(place, prob[:, j, :], ident[:, :])
                    if j % 4 == 3:
                        last.then_inc(tr_w.sem, 1)
                pe.wait_ge(wt_out.sem, wt_out.after(b))
                pe.wait_ge(exp_out.sem, exp_out.after(b))
                project(pa, 2, wt, tab[:, ODD_A, :]).then_inc(mm_wo.sem, 1)
                project(pa, 0, wt, tab[:, FWD_A, :]).then_inc(mm_we.sem, 1)

            def a_odd(b):
                pe.wait_ge(wo_out.sem, wo_out.after(b))
                project(pa, 2, ctx_a, tab[:, ODD_B, :]).then_inc(mm_bo.sem, 1)
                pe.wait_ge(prod_e.sem, prod_e.after(b))
                project(pa, 0, ctx_a, tab[:, ODD_C, :]).then_inc(mm_co.sem, 1)

            def a_aggregate(b):
                pe.wait_ge(prod_o.sem, prod_o.after(b))
                for h in range(2):
                    cols = slice(h * HALF, (h + 1) * HALF)
                    mm(pa[:, 2 + h, :], tab[:, AGG_1, :], p1[:, cols], start=True, stop=False)
                    mm(pa[:, 2 + h, :], tab[:, AGG_2, :], p2[:, cols], start=False, stop=False)
                    mm(pa[:, 2 + h, :], tab[:, AGG_3, :], p3[:, cols], start=False, stop=False)
                    last = mm(pa[:, 2 + h, :], tab[:, AGG_4, :], p4[:, cols], start=False, stop=True)
                last.then_inc(mm_agg.sem, 1)

            def r_experts_in(b, n, ln, weights, width):
                pe.wait_ge(ln_out[ln].sem, ln_out[ln].after(b))
                if n == 0:
                    if not (isinstance(b, int) and b == 0):
                        pe.wait_ge(x4_out.sem, x4_out.after(b - 1))
                else:
                    pe.wait_ge(av_out.sem, av_out.after(b))
                for j in range(KT):
                    place = pr[:, j // 4, (j % 4) * P:(j % 4 + 1) * P]
                    last = nc.tensor.transpose(place, xn_r[:, j * P:(j + 1) * P], ident[:, :])
                    if j % 4 == 3:
                        last.then_inc(tr_x[n].sem, 1)
                if n == 0:
                    if not (isinstance(b, int) and b == 0):
                        pe.wait_ge(midt_out[1].sem, midt_out[1].after(b - 1))
                else:
                    pe.wait_ge(x3_out.sem, x3_out.after(b))
                pe.wait_ge(xt_out[n].sem, xt_out[n].after(b))
                for j in range(KT):
                    last = mm(pr[:, 2, 0:width], xt[:, j * P:(j + 1) * P], weights[:, j, :],
                              start=(j == 0), stop=(j == KT - 1))
                last.then_inc(mm_ra[n].sem, 1)

            def r_experts_mid(b, n):
                pe.wait_ge(mid_out[n].sem, mid_out[n].after(b))
                nc.tensor.transpose(pr[:, 2, 256:256 + P], mid[:, :], ident[:, :])\
                    .then_inc(tr_mid[n].sem, 1)

            def r_base(b, h):
                for j in range(KT):
                    mm(pr[:, h, :], xt[:, j * P:(j + 1) * P], w_base[:, j, h * HALF:(h + 1) * HALF],
                       start=(j == 0), stop=False)

            def r_base_end(b):
                pe.wait_ge(midt_out[0].sem, midt_out[0].after(b))
                for h in range(2):
                    last = mm(pr[:, h, :], mid_t[:, :], w_b0[:, h * HALF:(h + 1) * HALF],
                              start=False, stop=True)
                last.then_inc(mm_ffn[0].sem, 1)

            def r_keys_values(b):
                pe.wait_ge(ctxr_in.sem, ctxr_in.after(b))
                pe.wait_ge(midt_out[0].sem, midt_out[0].after(b))
                project(pr, 2, ctx_r, w_att[:, 1, :]).then_inc(mm_k.sem, 1)
                pe.wait_ge(k_out.sem, k_out.after(b))
                project(pr, 2, ctx_r, w_att[:, 2, :]).then_inc(mm_v.sem, 1)

            def r_queries(b):
                pe.wait_ge(ln_out[2].sem, ln_out[2].after(b))
                pe.wait_ge(x2_out.sem, x2_out.after(b))
                project(pr, 0, xn_r, w_att[:, 0, :]).then_inc(mm_qq.sem, 1)

            def r_scores(b, g):
                if g == 0:
                    pe.wait_ge(qd_out.sem, qd_out.after(b))
                    pe.wait_ge(v_out.sem, v_out.after(b))
                if g >= 2:
                    pe.wait_ge(sc_in.sem, sc_in.after(b, g - 1))
                for i in range(GB):
                    blk = g * GB + i
                    last = mm(pr[:, 2 + g % 2, i * KEYS:(i + 1) * KEYS], q_diag[:, blk, :],
                              k_pad[:, blk * QB:blk * QB + KEYS], start=True, stop=True)
                last.then_inc(mm_sc.sem, 1)

            def r_attend(b, g):
                pe.wait_ge(sct_out.sem, sct_out.after(b, g + 1))
                if g == 0:
                    pe.wait_ge(vd_out.sem, vd_out.after(b))
                for i in range(GB):
                    blk = g * GB + i
                    col = (g % 2) * 256 + i * QB
                    for a in range(2):
                        last = mm(pr[64 * a:64 * a + 64, g // 2, col:col + QB], v_diag[:, blk, a, :],
                                  sc_t[:, blk, a * QB:(a + 1) * QB], start=True, stop=True)
                last.then_inc(mm_av.sem, 1)

            def r_output(b):
                pe.wait_ge(av_out.sem, av_out.after(b))
                pe.wait_ge(sc_in.sem, sc_in.after(b))
                project(pr, 2, xt, w_att[:, 3, :]).then_inc(mm_o.sem, 1)

            def r_delta(b):
                pe.wait_ge(midt_out[1].sem, midt_out[1].after(b))
                project(pr, 0, w_b1, mid_t[0:E1 * RANK, :]).then_inc(mm_ffn[1].sem, 1)

            def both(i, do_a, do_r):
                if do_a:
                    a_context(i)
                    a_query(i)
                r = i - 1
                if do_r:
                    r_experts_in(r, 0, 1, w_ra0, E0 + P)
                    r_base(r, 0)
                if do_a:
                    a_corr(i)
                if do_r:
                    r_experts_mid(r, 0)
                    r_base(r, 1)
                    r_base_end(r)
                    r_keys_values(r)
                    r_queries(r)
                if do_a:
                    a_weights(i)
                if do_r:
                    r_scores(r, 0)
                    r_scores(r, 1)
                if do_a:
                    a_odd(i)
                if do_r:
                    r_scores(r, 2)
                    r_attend(r, 0)
                    r_scores(r, 3)
                    r_attend(r, 1)
                if do_a:
                    a_aggregate(i)
                if do_r:
                    r_attend(r, 2)
                    r_attend(r, 3)
                    r_output(r)
                    r_experts_in(r, 1, 3, w_ra1, E1 + E1 * RANK)
                    r_experts_mid(r, 1)
                    r_delta(r)

            pe.wait_ge(const_in.sem, CONSTS_IN)
            both(0, True, False)
            with pe.Fori(1, BATCH) as i:
                both(i, True, True)
            both(BATCH, False, True)

        @block.scalar
        def _(act):
            def copy(dst, src):
                return nc.scalar.activation(dst, src, ACT.Copy)

            def a_spectra(b):
                act.wait_ge(mm_vb.sem, mm_vb.after(b))
                if not (isinstance(b, int) and b == 0):
                    act.wait_ge(prod_e.sem, prod_e.after(b - 1))
                copy(v_b[:, :], pa_lo).then_inc(vb_out.sem, 1)
                act.wait_ge(mm_vc.sem, mm_vc.after(b))
                copy(v_c[:, :], pa_hi).then_inc(vc_out.sem, 1)

            def a_query(b):
                act.wait_ge(mm_q.sem, mm_q.after(b))
                copy(q_spec[:, :], pa_lo).then_inc(q_out.sem, 1)

            def a_exp(b):
                for j in range(KT):
                    if j % 4 == 0:
                        act.wait_ge(negmax_out.sem, negmax_out.after(b, j // 4 + 1))
                    nc.scalar.activation(prob[:, j, :], pa[:, j // 4, (j % 4) * P:(j % 4 + 1) * P], ACT.Exp,
                                         bias=neg_max[:, j:j + 1]).then_inc(exp_out.sem, 1)

            def a_weights(b):
                for h in range(2):
                    act.wait_ge(tr_w.sem, tr_w.after(b, h + 1))
                    copy(wt[:, h * HALF:(h + 1) * HALF], pa[:, 2 + h, :]).then_inc(wt_out.sem, 1)
                act.wait_ge(mm_wo.sem, mm_wo.after(b))
                act.wait_ge(prod_q.sem, prod_q.after(b))
                copy(w_odd[:, :], pa_hi).then_inc(wo_out.sem, 1)

            def r_experts_xt(b, n):
                for h in range(2):
                    act.wait_ge(tr_x[n].sem, tr_x[n].after(b, h + 1))
                    if n == 1:
                        act.wait_ge(mm_o.sem, mm_o.after(b))
                    copy(xt[:, h * HALF:(h + 1) * HALF], pr[:, h, :]).then_inc(xt_out[n].sem, 1)

            def r_experts_exp(b, n, experts):
                act.wait_ge(gt[n].sem, gt[n].after(b, 5))
                nc.scalar.activation(lg_exp[:, 0:experts], lg[n][:, 0:experts], ACT.Exp, bias=lg_neg[:, :])\
                    .then_inc(gt_exp[n].sem, 1)

            def r_experts_mid(b, n, rows):
                act.wait_ge(tr_mid[n].sem, tr_mid[n].after(b))
                copy(mid_t[0:rows, :], pr[0:rows, 2, 256:256 + P]).then_inc(midt_out[n].sem, 1)

            def r_keys_values(b):
                act.wait_ge(mm_k.sem, mm_k.after(b))
                nc.scalar.activation(k_pad[:, PAD:PAD + D], pr_hi, ACT.Identity, bias=bias_att[:, 1:2])\
                    .then_inc(k_out.sem, 1)
                act.wait_ge(mm_v.sem, mm_v.after(b))
                if not (isinstance(b, int) and b == 0):
                    act.wait_ge(vt_out.sem, vt_out.after(b - 1))
                nc.scalar.activation(v_pad[:, PAD:PAD + D], pr_hi, ACT.Identity, bias=bias_att[:, 2:3])\
                    .then_inc(v_out.sem, 1)

            def r_queries(b):
                act.wait_ge(mm_qq.sem, mm_qq.after(b))
                for pair in range(4):
                    rows = slice(32 * pair, 32 * pair + 32)
                    source = pr_lo[rows, :].rearrange("p (n t) -> p n t", t=QB)
                    for a in range(2):
                        col = (2 * pair + a) * QB
                        nc.scalar.activation(q_diag[rows, :, col:col + QB], source, ACT.Identity,
                                             bias=bias_q[rows, a:a + 1], scale=par[rows, a:a + 1])\
                            .then_inc(qd_out.sem, 1)

            def r_value_blocks(b):
                if not (isinstance(b, int) and b == 0):
                    act.wait_ge(mm_av.sem, mm_av.after(b - 1))
                for odd in range(2):
                    act.wait_ge(vt_out.sem, vt_out.after(b, odd + 1))
                    for pair in range(4):
                        rows = slice(32 * pair, 32 * pair + 32)
                        place = v_diag[rows, :, :, pair * HD:(pair + 1) * HD]\
                            .rearrange("p (m o) a d -> p o m a d", o=2)[:, odd]
                        copy(place, v_t[rows, odd, :, :].rearrange("p m (a d) -> p m a d", a=2))\
                            .then_inc(vd_out.sem, 1)

            def r_exp(b, g):
                act.wait_ge(sc_less.sem, sc_less.after(b, 2 * g + 2))
                part = sc[:, g * GB:(g + 1) * GB, :]
                nc.scalar.activation(part, part, ACT.Exp, scale=ATT_SCALE).then_inc(sc_exp.sem, 1)

            def r_attended(b, h):
                act.wait_ge(mm_av.sem, mm_av.after(b, 2 * h + 2))
                copy(xt[:, h * HALF:(h + 1) * HALF], pr[:, h, :]).then_inc(av_out.sem, 1)

            def both(i, do_a, do_r):
                r = i - 1
                if do_a:
                    a_spectra(i)
                    a_query(i)
                if do_r:
                    r_experts_xt(r, 0)
                    r_experts_exp(r, 0, E0)
                    r_experts_mid(r, 0, P)
                if do_a:
                    a_exp(i)
                if do_r:
                    r_keys_values(r)
                    r_queries(r)
                if do_a:
                    a_weights(i)
                if do_r:
                    r_value_blocks(r)
                    for g in range(NG):
                        r_exp(r, g)
                        if g == 3:
                            r_attended(r, 0)
                    r_attended(r, 1)
                    r_experts_xt(r, 1)
                    r_experts_exp(r, 1, E1)
                    r_experts_mid(r, 1, E1 * RANK)

            act.wait_ge(const_in.sem, CONSTS_IN)
            act.wait_ge(const_set.sem, CONSTS_SET)
            both(0, True, False)
            with act.Fori(1, BATCH) as i:
                both(i, True, True)
            both(BATCH, False, True)

        @block.vector
        def _(dve):
            v = nc.vector

            def ln_stats(b, n, rows):
                for h in range(2):
                    v.bn_stats(bn[n][:, h, :], rows[:, h * HALF:(h + 1) * HALF]).then_inc(ln_bn[n].sem, 1)
                dve_wait(dve, ln_bn[n], ln_bn[n].after(b))
                v.bn_aggr(mv[n][:, :], bn[n][:, :, :]).then_inc(ln_mv[n].sem, 1)

            def ln_apply(b, n, rows, place):
                dve.wait_ge(ln_rs[n].sem, ln_rs[n].after(b))
                v.tensor_scalar(place[:, :], rows[:, :], mv[n][:, 0:1], rs_y[n][:, :],
                                ALU.subtract, ALU.mult).then_inc(ln_out[n].sem, 1)

            def a_norm_stats(b):
                dve.wait_ge(x_in.sem, x_in.after(b))
                ln_stats(b, 0, x_a)

            def a_norm_apply(b):
                if not (isinstance(b, int) and b == 0):
                    dve.wait_ge(mm_we.sem, mm_we.after(b - 1))
                ln_apply(b, 0, x_a, xn_a)

            def a_products(b):
                dve.wait_ge(q_out.sem, q_out.after(b))
                dve.wait_ge(vb_out.sem, vb_out.after(b))
                v.tensor_tensor(p1[:, :], q_spec[:, :], v_b[:, :], ALU.mult).then_inc(prod_q.sem, 1)
                dve.wait_ge(vc_out.sem, vc_out.after(b))
                v.tensor_tensor(p2[:, :], q_spec[:, :], v_c[:, :], ALU.mult).then_inc(prod_q.sem, 1)

            def a_top(b):
                for h in range(2):
                    dve_wait(dve, mm_corr, mm_corr.after(b, h + 1))
                    for j in range(4 * h, 4 * h + 4):
                        v.max(top8[:, j, :], pa[:, h, (j % 4) * P:(j % 4 + 1) * P]).then_inc(top_found.sem, 1)
                    for j in range(4 * h, 4 * h + 4):
                        if j % 4 == 0:
                            dve_wait(dve, top_found, top_found.after(b, j + 4))
                        v.match_replace(rest[:, j, :], top8[:, j, :], pa[:, h, (j % 4) * P:(j % 4 + 1) * P],
                                        GONE).then_inc(top_gone.sem, 1)
                    dve.wait_ge(top_gone.sem, top_gone.after(b, 4 * h + 4))
                    v.tensor_scalar(neg_max[:, 4 * h:4 * h + 4], top8[:, 4 * h:4 * h + 4, 0], -1.0, None,
                                    ALU.mult).then_inc(negmax_out.sem, 1)

            def a_ninth(b):
                dve.wait_ge(top_gone.sem, top_gone.after(b))
                v.tensor_reduce(ninth[:, :, 0], rest[:, :, :], AX_X, ALU.max).then_inc(ninth_found.sem, 1)
                dve_wait(dve, ninth_found, ninth_found.after(b))
                for j in range(KT):
                    v.match_replace(rest[:, j, :], ninth[:, j, :], rest[:, j, :], GONE)\
                        .then_inc(ninth_gone.sem, 1)
                for j in range(KT):
                    dve.wait_ge(ninth_gone.sem, ninth_gone.after(b, j + 1))
                    dve.wait_ge(exp_out.sem, exp_out.after(b, j + 1))
                    v.scalar_tensor_tensor(out=prob[:, j, :], in0=rest[:, j, :], scalar=GONE_MAX,
                                           in1=prob[:, j, :], op0=ALU.is_le, op1=ALU.mult,
                                           accum_out=psum_w[:, j:j + 1]).then_inc(prob_masked.sem, 1)
                dve.wait_ge(prob_masked.sem, prob_masked.after(b))
                v.reciprocal(rec_w[:, :], psum_w[:, :]).then_inc(rec_out.sem, 1)
                dve.wait_ge(rec_out.sem, rec_out.after(b))
                v.tensor_tensor(prob[:, :, :], prob[:, :, :],
                                rec_w[:, :].unsqueeze(2).to_broadcast([P, KT, P]), ALU.mult)\
                    .then_inc(prob_out.sem, 1)

            def a_products_even(b):
                dve.wait_ge(mm_we.sem, mm_we.after(b))
                v.tensor_tensor(p1[:, :], pa_lo, v_b[:, :], ALU.mult).then_inc(prod_e.sem, 1)
                v.tensor_tensor(p2[:, :], pa_lo, v_c[:, :], ALU.mult).then_inc(prod_e.sem, 1)

            def a_products_odd(b):
                dve.wait_ge(wo_out.sem, wo_out.after(b))
                dve.wait_ge(mm_bo.sem, mm_bo.after(b))
                v.tensor_tensor(p3, pa_hi, w_odd[:, :], ALU.mult).then_inc(prod_o.sem, 1)
                dve.wait_ge(mm_co.sem, mm_co.after(b))
                v.tensor_tensor(p4, pa_lo, w_odd[:, :], ALU.mult).then_inc(prod_o.sem, 1)

            def a_residual(b):
                dve.wait_ge(mm_agg.sem, mm_agg.after(b))
                if not (isinstance(b, int) and b == 0):
                    dve.wait_ge(x4_out.sem, x4_out.after(b - 1))
                v.tensor_tensor(x_r[:, :], pa_hi, x_a[:, :], ALU.add).then_inc(x1_out.sem, 1)

            def r_norm(b, n, before):
                if n == 1:
                    if not (isinstance(b, int) and b == 0):
                        dve.wait_ge(out_done.sem, out_done.after(b - 1))
                dve.wait_ge(before.sem, before.after(b))
                ln_stats(b, n, x_r)
                if n == 2:
                    dve.wait_ge(tr_x[0].sem, tr_x[0].after(b))
                if n == 3:
                    dve.wait_ge(mm_qq.sem, mm_qq.after(b))
                ln_apply(b, n, x_r, xn_r)

            def r_gates(b, n, experts, scale):
                g = gt[n]
                width = experts * RANK
                dve.wait_ge(mm_ra[n].sem, mm_ra[n].after(b))
                v.tensor_copy(lg[n][:, 0:experts], pr[:, 2, 0:experts]).then_inc(g.sem, 1)
                dve_wait(dve, g, g.after(b, 1))
                v.max(lg_top[:, :], lg[n][:, 0:E0]).then_inc(g.sem, 1)
                dve.wait_ge(g.sem, g.after(b, 2))
                v.tensor_copy(lg_pick[:, 0:2], lg_top[:, 0:2]).then_inc(g.sem, 1)
                dve_wait(dve, g, g.after(b, 3))
                v.match_replace(lg_mark[:, :], lg_pick[:, :], lg[n][:, :], TAKEN).then_inc(g.sem, 1)
                v.tensor_scalar(lg_neg[:, :], lg_top[:, 0:1], -1.0, None, ALU.mult).then_inc(g.sem, 1)
                dve.wait_ge(g.sem, g.after(b, 5))
                dve.wait_ge(gt_exp[n].sem, gt_exp[n].after(b))
                v.scalar_tensor_tensor(out=gate[:, 0:experts], in0=lg_mark[:, 0:experts], scalar=TAKEN_MIN,
                                       in1=lg_exp[:, 0:experts], op0=ALU.is_ge, op1=ALU.mult,
                                       accum_out=gate_sum[:, :]).then_inc(g.sem, 1)
                dve.wait_ge(g.sem, g.after(b, 6))
                v.reciprocal(gate_rec[:, :], gate_sum[:, :]).then_inc(g.sem, 1)
                dve.wait_ge(g.sem, g.after(b, 7))
                v.tensor_scalar(gate[:, 0:experts], gate[:, 0:experts], gate_rec[:, :], scale,
                                ALU.mult, ALU.mult).then_inc(g.sem, 1)
                dve.wait_ge(g.sem, g.after(b, 8))
                v.tensor_tensor(mid[:, 0:width].rearrange("p (e r) -> p e r", r=RANK),
                                pr[:, 2, experts:experts + width].rearrange("p (e r) -> p e r", r=RANK),
                                gate[:, 0:experts].unsqueeze(2).to_broadcast([P, experts, RANK]), ALU.mult)\
                    .then_inc(mid_out[n].sem, 1)

            def r_base(b):
                dve.wait_ge(mm_ffn[0].sem, mm_ffn[0].after(b))
                dve.wait_ge(bias_added.sem, bias_added.after(b))
                v.tensor_tensor(x_r[:, :], pr_lo, x_r[:, :], ALU.add).then_inc(x2_out.sem, 1)

            def r_values(b):
                dve.wait_ge(v_out.sem, v_out.after(b))
                if not (isinstance(b, int) and b == 0):
                    dve.wait_ge(mm_av.sem, mm_av.after(b - 1))
                for odd in range(2):
                    v.transpose(v_t[:, odd, :, :].rearrange("p m k -> p (m k)"),
                                v_pad[:, odd * QB:odd * QB + D]).then_inc(vt_out.sem, 1)

            def r_scores(b, g):
                part = sc[:, g * GB:(g + 1) * GB, :]
                dve.wait_ge(mm_sc.sem, mm_sc.after(b, g + 1))
                v.tensor_tensor(part, pr[:, 2 + g % 2, :].rearrange("p (n k) -> p n k", k=KEYS),
                                band_mask[:, :].unsqueeze(1).to_broadcast([P, GB, KEYS]), ALU.add)\
                    .then_inc(sc_in.sem, 1)
                dve.wait_ge(sc_in.sem, sc_in.after(b, g + 1))
                blocks = slice(g * GB, (g + 1) * GB)
                v.tensor_reduce(sc_max[:, blocks], part, AX_X, ALU.max).then_inc(sc_less.sem, 1)
                dve.wait_ge(sc_less.sem, sc_less.after(b, 2 * g + 1))
                v.tensor_tensor(part, part, sc_max[:, blocks].unsqueeze(2).to_broadcast([P, GB, KEYS]),
                                ALU.subtract).then_inc(sc_less.sem, 1)

            def r_probs(b, g):
                part = sc[:, g * GB:(g + 1) * GB, :]
                blocks = slice(g * GB, (g + 1) * GB)
                dve.wait_ge(sc_exp.sem, sc_exp.after(b, g + 1))
                v.tensor_reduce(sc_sum[:, blocks], part, AX_X, ALU.add).then_inc(sc_norm.sem, 1)
                dve.wait_ge(sc_norm.sem, sc_norm.after(b, 3 * g + 1))
                v.reciprocal(sc_rec[:, blocks], sc_sum[:, blocks]).then_inc(sc_norm.sem, 1)
                dve.wait_ge(sc_norm.sem, sc_norm.after(b, 3 * g + 2))
                v.tensor_tensor(part, part, sc_rec[:, blocks].unsqueeze(2).to_broadcast([P, GB, KEYS]),
                                ALU.mult).then_inc(sc_norm.sem, 1)
                dve.wait_ge(sc_norm.sem, sc_norm.after(b, 3 * g + 3))
                if g == 0:
                    dve.wait_ge(vd_out.sem, vd_out.after(b))
                v.transpose(sc_t[:, blocks, :].rearrange("p n k -> p (n k)"),
                            part.rearrange("p n k -> p (n k)")).then_inc(sct_out.sem, 1)

            def r_attention_residual(b):
                dve.wait_ge(mm_o.sem, mm_o.after(b))
                v.scalar_tensor_tensor(out=x_r[:, :], in0=pr_hi, scalar=bias_att[:, 3:4], in1=x_r[:, :],
                                       op0=ALU.add, op1=ALU.add).then_inc(x3_out.sem, 1)

            def r_result(b):
                dve.wait_ge(mm_ffn[1].sem, mm_ffn[1].after(b))
                v.tensor_tensor(xn_r[:, :], pr_lo, x_r[:, :], ALU.add).then_inc(x4_out.sem, 1)

            def both(i, do_a, do_r):
                r = i - 1
                if do_a:
                    a_norm_stats(i)
                if do_a:
                    a_norm_apply(i)
                if do_r:
                    r_norm(r, 1, x1_out)
                if do_a:
                    a_products(i)
                if do_r:
                    r_gates(r, 0, E0, SCALE0)
                if do_a:
                    a_top(i)
                    a_ninth(i)
                if do_r:
                    r_base(r)
                    r_norm(r, 2, x2_out)
                    r_values(r)
                if do_a:
                    a_products_even(i)
                if do_r:
                    r_scores(r, 0)
                if do_a:
                    a_products_odd(i)
                if do_r:
                    r_scores(r, 1)
                    r_probs(r, 0)
                    r_scores(r, 2)
                    r_probs(r, 1)
                    r_scores(r, 3)
                    r_probs(r, 2)
                    r_probs(r, 3)
                    r_attention_residual(r)
                    r_norm(r, 3, x3_out)
                    r_gates(r, 1, E1, SCALE1)
                    r_result(r)
                if do_a:
                    a_residual(i)

            v.memset(ninth[:, :, :], GONE).then_inc(const_set.sem, 1)
            v.memset(lg[0][:, :], GONE).then_inc(const_set.sem, 1)
            v.memset(lg[1][:, :], GONE).then_inc(const_set.sem, 1)
            v.memset(lg_pick[:, :], GONE).then_inc(const_set.sem, 1)
            v.memset(k_pad[:, :], 0.0).then_inc(const_set.sem, 1)
            v.memset(v_pad[:, :], 0.0).then_inc(const_set.sem, 1)
            v.memset(q_diag[:, :, :], 0.0).then_inc(const_set.sem, 1)
            v.memset(v_diag[:, :, :, :], 0.0).then_inc(const_set.sem, 1)
            dve.wait_ge(const_in.sem, CONSTS_IN)
            v.tensor_scalar(bias_q[:, :], par[:, :], bias_att[:, 0:1], None, ALU.mult)\
                .then_inc(const_set.sem, 1)
            dve.wait_ge(const_set.sem, CONSTS_SET)
            both(0, True, False)
            with dve.Fori(1, BATCH) as i:
                both(i, True, True)
            both(BATCH, False, True)

        @block.gpsimd
        def _(pool):
            g = nc.gpsimd

            def rsqrt(b, n):
                var, t, y, steps = rs_v[n], rs_t[n], rs_y[n], ln_rs[n]
                pool_wait(pool, ln_mv[n], ln_mv[n].after(b))
                g.tensor_scalar(var[:, :], mv[n][:, 1:2], 1e-5, None, ALU.add).then_inc(steps.sem, 1)
                pool_wait(pool, steps, steps.after(b, 1))
                g.tensor_scalar(y[:, :].bitcast(I32), var[:, :].bitcast(I32), -0.5, float(RSQRT_MAGIC),
                                ALU.mult, ALU.add).then_inc(steps.sem, 1)
                for k in range(RSQRT_NEWTON):
                    at = 2 + 4 * k
                    pool.wait_ge(steps.sem, steps.after(b, at))
                    g.tensor_tensor(t[:, :], y[:, :], y[:, :], ALU.mult).then_inc(steps.sem, 1)
                    pool.wait_ge(steps.sem, steps.after(b, at + 1))
                    g.tensor_tensor(t[:, :], t[:, :], var[:, :], ALU.mult).then_inc(steps.sem, 1)
                    pool_wait(pool, steps, steps.after(b, at + 2))
                    g.tensor_scalar(t[:, :], t[:, :], -0.5, 1.5, ALU.mult, ALU.add).then_inc(steps.sem, 1)
                    pool.wait_ge(steps.sem, steps.after(b, at + 3))
                    g.tensor_tensor(y[:, :], y[:, :], t[:, :], ALU.mult).then_inc(steps.sem, 1)

            def add_bias(b):
                pool.wait_ge(ln_out[1].sem, ln_out[1].after(b))
                g.tensor_tensor(x_r[:, :], x_r[:, :], bias_base[:, :], ALU.add).then_inc(bias_added.sem, 1)

            def both(i, do_a, do_r):
                r = i - 1
                if do_a:
                    rsqrt(i, 0)
                if do_r:
                    rsqrt(r, 1)
                    add_bias(r)
                    rsqrt(r, 2)
                    rsqrt(r, 3)

            pool.wait_ge(const_in.sem, CONSTS_IN)
            pool.wait_ge(const_set.sem, CONSTS_SET)
            both(0, True, False)
            with pool.Fori(1, BATCH) as i:
                both(i, True, True)
            both(BATCH, False, True)


_OUTS = [((32, 128, 1024), "float32")]


def kernel(**inputs):
    import concourse.bacc as bacc
    from concourse.bass_utils import run_bass_kernel_spmd as run

    f = {k: np.asarray(v) for k, v in inputs.items()}

    def tiles(w):
        return w.T.reshape(8, 128, -1).transpose(1, 0, 2)

    head_order = [2 * pair + a for a in range(2) for pair in range(4)]
    channels = np.concatenate([np.arange(16 * h, 16 * h + 16) for h in head_order])
    key = np.arange(32)[None, :] - (np.arange(128) % 16)[:, None]
    odd_head = (np.arange(128) // 16) % 2
    data = {
        "x": f["x"],
        "ctx_in": f["ctx_4096"],
        "spectra": spectral_tables(),
        "identity": np.eye(128, dtype=np.float32),
        "band": np.where((key >= 0) & (key < 16), 0.0, GONE).astype(np.float32),
        "parity": np.stack([1 - odd_head, odd_head], 1).astype(np.float32),
        "base_w": tiles(f["L0_ffn_W_base"]),
        "base_b": f["L0_ffn_b_base"],
        "ra0": tiles(np.concatenate([f["L0_ffn_W_router"], f["L0_ffn_A_stack"].reshape(128, 1024)])),
        "b0": f["L0_ffn_B_stack"].transpose(0, 2, 1).reshape(128, 1024),
        "wqkvo": np.stack([f["L1_xattn_Wq"].T, f["L1_xattn_Wk"].T, f["L1_xattn_Wv"].T,
                           f["L1_xattn_Wo"].T[channels]], 1),
        "biases": np.stack([f["L1_xattn_bq"], f["L1_xattn_bk"], f["L1_xattn_bv"], f["L1_xattn_bo"]], 1),
        "ra1": tiles(np.concatenate([f["L1_ffn_Wr"], f["L1_ffn_A"].reshape(64, 1024)])),
        "b1": f["L1_ffn_B"].transpose(0, 2, 1).reshape(64, 1024),
    }
    nc = bacc.Bacc("TRN2", target_bir_lowering=False, num_devices=1)
    arrays, args = {}, []
    for name, a in data.items():
        a = np.ascontiguousarray(a)
        arrays[f"in_{name}"] = a
        args.append(nc.dram_tensor(f"in_{name}", a.shape, mybir.dt.from_np(a.dtype), kind="ExternalInput").ap())
    shape, dtype = _OUTS[0]
    args.append(nc.dram_tensor("out_0", shape, mybir.dt.from_np(np.dtype(dtype)), kind="ExternalOutput").ap())
    build(nc, *args)
    r = run(nc, [arrays], core_ids=[0])
    return r.results[0]["out_0"]
```

```python
import math
from contextlib import ExitStack

import numpy as np

import concourse.bass as bass
from concourse import mybir

F32 = mybir.dt.float32
I32 = mybir.dt.int32
F16 = mybir.dt.float16
BF16 = mybir.dt.bfloat16
ALU = mybir.AluOpType
ACT = mybir.ActivationFunctionType
AX_X = mybir.AxisListType.X

P = 128
GONE = -3.0e38
GONE_MAX = -2.9e38
TAKEN = 3.0e38
TAKEN_MIN = 2.9e38
RSQRT_MAGIC = 0x5F3759DF
RSQRT_ROUNDS = 2
RSQRT_STEPS = 2 + 4 * RSQRT_ROUNDS
W_SCALE = 256.0


class Signal:

    def __init__(self, sem, per):
        self.sem = sem
        self.per = per

    def after(self, b, k=None):
        return b * self.per + (self.per if k is None else k)


def spectral_tables():
    n = P
    half = n // 2
    t = np.arange(n, dtype=np.float64)
    k = np.arange(half, dtype=np.float64)
    even = 2.0 * np.pi * np.outer(t, k) / n
    odd = 2.0 * np.pi * np.outer(t, k + 0.5) / n
    alt = (-1.0) ** t

    fwd_a = np.concatenate([np.cos(even), -np.sin(even)], 1)
    fwd_a[:, half] = alt
    fwd_b = np.concatenate([np.cos(even), np.cos(even)], 1)
    fwd_b[:, half] = alt
    fwd_c = np.concatenate([-np.sin(even), -np.sin(even)], 1)
    fwd_c[:, 0] = 0.0
    fwd_c[:, half] = 0.0
    odd_a = np.concatenate([np.cos(odd), -np.sin(odd)], 1)
    odd_b = np.concatenate([np.cos(odd), np.cos(odd)], 1)
    odd_c = np.concatenate([-np.sin(odd), -np.sin(odd)], 1)

    def minus_last(f):
        f = f.copy()
        f[n - 1] -= f.sum(0)
        return f

    fwd_b, fwd_c, odd_b, odd_c = map(minus_last, (fwd_b, fwd_c, odd_b, odd_c))
    fwd_c[n - 1, 0] = 1.0

    scale = np.full((half, 1), 2.0 / n)
    scale[0] = 1.0 / n
    cos_e, sin_e = scale * np.cos(even).T, scale * np.sin(even).T
    corr_1 = np.concatenate([cos_e, -sin_e])
    corr_2 = np.concatenate([sin_e, cos_e])
    corr_1[half] = alt / n
    corr_2[0] = 0.0
    corr_2[half] = 0.0
    agg_1 = np.concatenate([cos_e, sin_e]) / 2
    agg_2 = np.concatenate([-sin_e, cos_e]) / 2
    agg_1[half] = alt / n / 2
    agg_2[0] = 1.0
    agg_2[half] = 0.0
    cos_o, sin_o = np.cos(odd).T * (1.0 / n), np.sin(odd).T * (1.0 / n)
    agg_3 = np.concatenate([cos_o, sin_o])
    agg_4 = np.concatenate([-sin_o, cos_o])
    tables = [fwd_a, fwd_b, fwd_c, odd_a, odd_b, odd_c, corr_1, corr_2, agg_1, agg_2, agg_3, agg_4]
    return np.stack([m.astype(np.float32) for m in tables], 1)


(FWD_A, FWD_B, FWD_C, ODD_A, ODD_B, ODD_C, CORR_1, CORR_2, AGG_1, AGG_2, AGG_3, AGG_4) = range(12)


def first(b):
    return isinstance(b, int) and b == 0


def words(t):
    v = t.bitcast(F16)
    names = " ".join("abc"[:len(v.shape) - 1])
    return v.rearrange(f"{names} (n two) -> {names} n two", two=2)


LO, HI = 0, 1


def build(nc, x, ctx_in, spectra, identity, band, parity, base_w, base_b, ra0, b0, wqkvo, biases,
          ra1, b1, out):
    BATCH, _, D = x.shape
    KT = D // P
    HALF = D // 2
    E0, E1 = 8, 4
    RANK = 16
    SCALE0, SCALE1 = 32.0 / RANK, 16.0 / math.sqrt(16.0)
    HEADS, WINDOW = 8, 16
    HD = P // HEADS
    QB = 16
    NBLK = D // QB
    KEYS = 2 * QB
    PAD = WINDOW // 2
    NG = 4
    GB = NBLK // NG
    GW = GB * QB
    ATT_SCALE = HD ** -0.5
    TOPK = int(2 * np.log(P))
    assert TOPK == 9 and D == 1024

    ctx = ExitStack()
    with ctx:
        def sb(name, shape, dt=F32):
            return ctx.enter_context(nc.sbuf_tensor(name, shape, dt))

        def signal(name, per=1):
            return Signal(ctx.enter_context(nc.semaphore(name)), per)

        tab = sb("tab", [P, 12, P])
        ident = sb("ident", [P, P])
        ident_bf = sb("ident_bf", [P, P], BF16)
        band_mask = sb("band_mask", [P, KEYS])
        band_bf = sb("band_bf", [P, GB, KEYS], BF16)
        par = sb("par", [P, 2])
        w_base_h = sb("w_base_h", [P, KT, D], F16)
        w_base_l = sb("w_base_l", [P, KT, D], F16)
        bias_base = sb("bias_base", [P, D])
        w_ra0_h = sb("w_ra0_h", [P, KT, E0 + P], F16)
        w_ra0_l = sb("w_ra0_l", [P, KT, E0 + P], F16)
        w_b0 = sb("w_b0", [P, D])
        w_att = sb("w_att", [P, 4, P])
        bias_att = sb("bias_att", [P, 4])
        w_ra1 = sb("w_ra1", [P, KT, E1 + E1 * RANK])
        w_b1 = sb("w_b1", [E1 * RANK, D])

        x_a = sb("x_a", [P, D])
        ctx_a = sb("ctx_a", [P, D])
        xn_a = sb("xn_a", [P, D])
        wt = xn_a
        q_spec = sb("q_spec", [P, D])
        w_odd = q_spec
        v_b = sb("v_b", [P, D])
        v_c = sb("v_c", [P, D])
        rest = sb("rest", [P, KT, P])
        rest_flat = rest[:, :, :].rearrange("p a b -> p (a b)")
        prob = sb("prob", [P, KT, P])
        prob_flat = prob[:, :, :].rearrange("p a b -> p (a b)")
        c1, c2 = q_spec, rest_flat
        p1, p2, p3, p4 = v_b, v_c, rest_flat, prob_flat
        top8 = sb("top8", [P, KT, 8])
        ninth = sb("ninth", [P, KT, 8])
        neg_max = sb("neg_max", [P, KT])
        psum_w = sb("psum_w", [P, KT])
        rec_w = sb("rec_w", [P, KT])

        x_b = sb("x_b", [P, D])
        ctx_b = sb("ctx_b", [P, D])
        xn_b = sb("xn_b", [P, D])
        even_words = sb("even_words", [P, D])
        xt_h = even_words[:, :].bitcast(F16)[:, 0:D]
        xt_l = even_words[:, :].bitcast(F16)[:, D:2 * D]
        k_h = sb("k_h", [P, D + 2 * PAD], F16)
        k_l = sb("k_l", [P, D + 2 * PAD], F16)
        v_pad = sb("v_pad", [P, D + 2 * PAD])
        q_diag = sb("q_diag", [P, NBLK, P])
        v_diag = sb("v_diag", [P, NBLK, 2, P // 2])

        x_c = sb("x_c", [P, D])
        sc = sb("sc", [P, 2, GB, KEYS])
        p_hl = sb("p_hl", [P, 2, GB, KEYS])
        sc_t = sb("sc_t", [P, 2, GB, KEYS])
        xn_c = sb("xn_c", [P, D])
        sc_max = sb("sc_max", [P, NBLK])
        sc_sum = sb("sc_sum", [P, NBLK])
        sc_rec = sb("sc_rec", [P, NBLK])

        q_hl = sc[:, :, :, :].rearrange("p a n k -> p (a n k)")
        v_t = [even_words[:, :], p_hl[:, :, :, :].rearrange("p a n k -> p (a n k)")]
        xt_c = sc_t[:, :, :, :].rearrange("p a n k -> p (a n k)")
        at = xn_c

        lg = [sb(f"lg{n}", [P, 16]) for n in range(2)]
        lg_top = [sb(f"lg_top{n}", [P, 8]) for n in range(2)]
        lg_pick = [sb(f"lg_pick{n}", [P, 8]) for n in range(2)]
        lg_mark = [sb(f"lg_mark{n}", [P, 16]) for n in range(2)]
        lg_neg = [sb(f"lg_neg{n}", [P, 1]) for n in range(2)]
        lg_exp = [sb(f"lg_exp{n}", [P, E0]) for n in range(2)]
        gate = [sb(f"gate{n}", [P, E0]) for n in range(2)]
        gate_sum = [sb(f"gate_sum{n}", [P, 1]) for n in range(2)]
        gate_rec = [sb(f"gate_rec{n}", [P, 1]) for n in range(2)]
        mid = [sb(f"mid{n}", [P, [P, E1 * RANK][n]]) for n in range(2)]
        mid_t = [sb(f"mid_t{n}", [[P, E1 * RANK][n], P]) for n in range(2)]

        bn = [sb(f"bn{n}", [P, 2, 6]) for n in range(4)]
        mv = [sb(f"mv{n}", [P, 2]) for n in range(4)]
        rs_v = [sb(f"rs_v{n}", [P, 1]) for n in range(4)]
        rs_t = [sb(f"rs_t{n}", [P, 1]) for n in range(4)]
        rs_u = [sb(f"rs_u{n}", [P, 1]) for n in range(4)]
        rs_y = [sb(f"rs_y{n}", [P, 1]) for n in range(4)]
        idle_dve = sb("idle_dve", [P, 1])
        idle_pool = sb("idle_pool", [P, 1])

        def psum(name, banks):
            return ctx.enter_context(nc.psum_tensor(name, [P, banks, HALF], F32))

        def flat(t):
            return t.rearrange("p a b -> p (a b)")

        pa = psum("pa", 4)
        pb = psum("pb", 2)
        pc = psum("pc", 2)
        pa_lo, pa_hi = flat(pa[:, 0:2, :]), flat(pa[:, 2:4, :])
        pb_all, pc_all = flat(pb[:, :, :]), flat(pc[:, :, :])
        MID_AT = 256

        tab_in = signal("tab_in")
        const_in = signal("const_in")
        w_in = signal("w_in")
        const_set = signal("const_set")
        diag_set = signal("diag_set")
        w_hi = signal("w_hi")
        w_lo = signal("w_lo")
        x_in = signal("x_in", 16)
        ctxa_in = signal("ctxa_in", 16)
        ctxb_in = signal("ctxb_in", 16)
        out_done = signal("out_done", 16)
        ln_bn = [signal(f"ln_bn{n}", 2) for n in range(4)]
        ln_mv = [signal(f"ln_mv{n}") for n in range(4)]
        ln_rs = [signal(f"ln_rs{n}", RSQRT_STEPS) for n in range(4)]
        ln_out = [signal(f"ln_out{n}") for n in range(4)]
        mm_vb = signal("mm_vb")
        mm_vc = signal("mm_vc")
        mm_q = signal("mm_q")
        vb_out = signal("vb_out")
        vc_out = signal("vc_out")
        q_out = signal("q_out")
        prod_q = signal("prod_q", 2)
        mm_corr = signal("mm_corr", 2)
        top_found = signal("top_found", KT)
        top_gone = signal("top_gone", KT)
        negmax_out = signal("negmax_out", 2)
        ninth_found = signal("ninth_found")
        ninth_gone = signal("ninth_gone", KT)
        exp_out = signal("exp_out", KT)
        prob_masked = signal("prob_masked", KT)
        rec_out = signal("rec_out")
        prob_out = signal("prob_out")
        tr_w = signal("tr_w", 2)
        wt_out = signal("wt_out", 2)
        mm_we = signal("mm_we")
        mm_wo = signal("mm_wo")
        wo_out = signal("wo_out")
        prod_e = signal("prod_e", 2)
        mm_bo = signal("mm_bo")
        mm_co = signal("mm_co")
        prod_o = signal("prod_o", 2)
        mm_agg = signal("mm_agg")
        x1_out = signal("x1_out")
        tr_x = [signal(f"tr_x{n}", 2) for n in range(2)]
        xt_out = [signal(f"xt_out{n}", 2) for n in range(2)]
        xtl_out = signal("xtl_out", 2)
        mm_ra = [signal(f"mm_ra{n}") for n in range(2)]
        gt = [signal(f"gt{n}", 8) for n in range(2)]
        gt_exp = [signal(f"gt_exp{n}") for n in range(2)]
        mid_out = [signal(f"mid_out{n}") for n in range(2)]
        tr_mid = [signal(f"tr_mid{n}") for n in range(2)]
        midt_out = [signal(f"midt_out{n}") for n in range(2)]
        mm_ffn = [signal(f"mm_ffn{n}") for n in range(2)]
        bias_added = signal("bias_added")
        x2_out = signal("x2_out")
        x2_moved = signal("x2_moved")
        x4_out = signal("x4_out")
        mm_k = signal("mm_k")
        mm_v = signal("mm_v")
        mm_qq = signal("mm_qq")
        kh_out = signal("kh_out")
        kl_out = signal("kl_out")
        vh_out = signal("vh_out")
        vl_out = signal("vl_out")
        qh_out = signal("qh_out")
        ql_out = signal("ql_out")
        vt_out = signal("vt_out", 2)
        vd_out = signal("vd_out", 8)
        qd_out = signal("qd_out", HEADS)
        mm_sc = signal("mm_sc", NG)
        max_out = signal("max_out", NG)
        sc_in = signal("sc_in", NG)
        sc_exp = signal("sc_exp", NG)
        sum_out = signal("sum_out", NG)
        srec_out = signal("srec_out", NG)
        p_out = signal("p_out", NG)
        ph_out = signal("ph_out", NG)
        pl_out = signal("pl_out", NG)
        pt_out = signal("pt_out", NG)
        mm_av = signal("mm_av", NG)
        av_out = signal("av_out", 2 * NG)
        mm_o = signal("mm_o")
        x3_out = signal("x3_out")

        tables = [(tab, spectra), (ident, identity), (band_mask, band), (par, parity)]
        consts = [(w_b0, b0), (w_att, wqkvo), (bias_att, biases), (w_ra1, ra1), (w_b1, b1)]
        TABLES_IN = 16 * len(tables)
        CONSTS_IN = 16 * (len(consts) + 1)
        CONSTS_SET = 9
        WEIGHTS_SPLIT = 2

        base_f32 = v_diag[:, :, :, :].rearrange("p n a c -> p (n a c)")
        ra0_f32 = q_diag[:, :, :].rearrange("p n c -> p (n c)")[:, 0:KT * (E0 + P)]

        def dve_wait(dve, signal, value):
            dve.wait_ge(signal.sem, value)
            nc.vector.memset(idle_dve[:, :], 0.0)

        block = ctx.enter_context(nc.Block())

        @block.sync
        def _(sp):
            def load_x(b):
                if not first(b):
                    sp.wait_ge(x1_out.sem, x1_out.after(b - 1))
                sp.dma_start(x_a[:, :], x[b]).then_inc(x_in.sem, 16)

            def load_ctx_a(b):
                if not first(b):
                    sp.wait_ge(mm_co.sem, mm_co.after(b - 1))
                sp.dma_start(ctx_a[:, :], ctx_in[b]).then_inc(ctxa_in.sem, 16)

            def load_ctx_b(b):
                if not first(b):
                    sp.wait_ge(mm_v.sem, mm_v.after(b - 1))
                sp.dma_start(ctx_b[:, :], ctx_in[b]).then_inc(ctxb_in.sem, 16)

            def store(b):
                sp.wait_ge(x4_out.sem, x4_out.after(b))
                sp.dma_start(out[b], xn_c[:, :]).then_inc(out_done.sem, 16)

            load_ctx_a(0)
            sp.dma_start(tab[:], spectra).then_inc(tab_in.sem, 16)
            load_x(0)
            for place, source in tables[1:]:
                sp.dma_start(place[:], source).then_inc(tab_in.sem, 16)
            sp.dma_start(base_f32, base_w.rearrange("p k n -> p (k n)")).then_inc(w_in.sem, 16)
            sp.dma_start(ra0_f32, ra0.rearrange("p k n -> p (k n)")).then_inc(w_in.sem, 16)
            for place, source in consts:
                sp.dma_start(place[:], source).then_inc(const_in.sem, 16)
            sp.dma_start(bias_base[:, :], base_b.partition_broadcast(P)).then_inc(const_in.sem, 16)
            load_ctx_b(0)
            load_ctx_a(1)
            load_x(1)
            load_ctx_b(1)
            load_ctx_a(2)
            load_x(2)
            with sp.Fori(2, BATCH - 1) as i:
                load_ctx_b(i)
                load_ctx_a(i + 1)
                store(i - 2)
                load_x(i + 1)
            load_ctx_b(BATCH - 1)
            store(BATCH - 3)
            store(BATCH - 2)
            store(BATCH - 1)
            sp.wait_ge(out_done.sem, out_done.after(BATCH - 1))

        @block.tensor
        def _(pe):
            mm = nc.tensor.matmul

            def project(place, n, moving, lhsT):
                for h in range(2):
                    last = mm(place[:, n + h, :], lhsT, moving[:, h * HALF:(h + 1) * HALF],
                              start=True, stop=True)
                return last

            def a_context(b):
                pe.wait_ge(ctxa_in.sem, ctxa_in.after(b))
                if not first(b):
                    pe.wait_ge(prod_o.sem, prod_o.after(b - 1))
                project(pa, 0, ctx_a, tab[:, FWD_B, :]).then_inc(mm_vb.sem, 1)
                if not first(b):
                    pe.wait_ge(x1_out.sem, x1_out.after(b - 1))
                project(pa, 2, ctx_a, tab[:, FWD_C, :]).then_inc(mm_vc.sem, 1)

            def a_query(b):
                pe.wait_ge(vb_out.sem, vb_out.after(b))
                pe.wait_ge(ln_out[0].sem, ln_out[0].after(b))
                project(pa, 0, xn_a, tab[:, FWD_A, :]).then_inc(mm_q.sem, 1)

            def a_corr(b):
                pe.wait_ge(prod_q.sem, prod_q.after(b))
                pe.wait_ge(q_out.sem, q_out.after(b))
                for j in range(KT):
                    place = pa[:, j // 4, (j % 4) * P:(j % 4 + 1) * P]
                    mm(place, c1[:, j * P:(j + 1) * P], tab[:, CORR_1, :], start=True, stop=False)
                    last = mm(place, c2[:, j * P:(j + 1) * P], tab[:, CORR_2, :], start=False, stop=True)
                    if j % 4 == 3:
                        last.then_inc(mm_corr.sem, 1)

            def a_weights(b):
                pe.wait_ge(prob_out.sem, prob_out.after(b))
                pe.wait_ge(vc_out.sem, vc_out.after(b))
                for j in range(KT):
                    place = pa[:, 2 + j // 4, (j % 4) * P:(j % 4 + 1) * P]
                    last = nc.tensor.transpose(place, prob[:, j, :], ident[:, :])
                    if j % 4 == 3:
                        last.then_inc(tr_w.sem, 1)
                pe.wait_ge(wt_out.sem, wt_out.after(b))
                pe.wait_ge(exp_out.sem, exp_out.after(b))
                project(pa, 2, wt, tab[:, ODD_A, :]).then_inc(mm_wo.sem, 1)
                project(pa, 0, wt, tab[:, FWD_A, :]).then_inc(mm_we.sem, 1)

            def a_odd(b):
                pe.wait_ge(wo_out.sem, wo_out.after(b))
                project(pa, 2, ctx_a, tab[:, ODD_B, :]).then_inc(mm_bo.sem, 1)
                pe.wait_ge(prod_e.sem, prod_e.after(b))
                project(pa, 0, ctx_a, tab[:, ODD_C, :]).then_inc(mm_co.sem, 1)

            def a_aggregate(b):
                pe.wait_ge(prod_o.sem, prod_o.after(b))
                for h in range(2):
                    cols = slice(h * HALF, (h + 1) * HALF)
                    mm(pa[:, 2 + h, :], tab[:, AGG_1, :], p1[:, cols], start=True, stop=False)
                    mm(pa[:, 2 + h, :], tab[:, AGG_2, :], p2[:, cols], start=False, stop=False)
                    mm(pa[:, 2 + h, :], tab[:, AGG_3, :], p3[:, cols], start=False, stop=False)
                    last = mm(pa[:, 2 + h, :], tab[:, AGG_4, :], p4[:, cols], start=False, stop=True)
                last.then_inc(mm_agg.sem, 1)

            def rows_to_features(b, n, ln, source, place):
                pe.wait_ge(ln_out[ln].sem, ln_out[ln].after(b))
                if n == 0:
                    if not first(b):
                        pe.wait_ge(ql_out.sem, ql_out.after(b - 1))
                else:
                    pe.wait_ge(x3_out.sem, x3_out.after(b))
                for j in range(KT):
                    last = nc.tensor.transpose(place[:, j // 4, (j % 4) * P:(j % 4 + 1) * P],
                                               source[:, j * P:(j + 1) * P], ident[:, :])
                    if j % 4 == 3:
                        last.then_inc(tr_x[n].sem, 1)

            def b_router(b):
                pe.wait_ge(xtl_out.sem, xtl_out.after(b))
                n = 0
                for j in range(KT):
                    cols = slice(j * P, (j + 1) * P)
                    for rows, weights in ((xt_h, w_ra0_h), (xt_h, w_ra0_l), (xt_l, w_ra0_h)):
                        n += 1
                        last = mm(pb[:, 0, 0:E0 + P], rows[:, cols], weights[:, j, :],
                                  start=(n == 1), stop=(n == 3 * KT))
                last.then_inc(mm_ra[0].sem, 1)

            def b_base(b, h):
                if h == 0:
                    pe.wait_ge(midt_out[0].sem, midt_out[0].after(b))
                for j in range(KT):
                    cols = slice(j * P, (j + 1) * P)
                    for m, (rows, weights) in enumerate(((xt_h, w_base_h), (xt_h, w_base_l), (xt_l, w_base_h))):
                        mm(pb[:, h, :], rows[:, cols], weights[:, j, h * HALF:(h + 1) * HALF],
                           start=(j == 0 and m == 0), stop=False)

            def b_base_end(b):
                for h in range(2):
                    last = mm(pb[:, h, :], mid_t[0][:, :], w_b0[:, h * HALF:(h + 1) * HALF],
                              start=False, stop=True)
                last.then_inc(mm_ffn[0].sem, 1)

            def b_mid(b):
                pe.wait_ge(mid_out[0].sem, mid_out[0].after(b))
                nc.tensor.transpose(pb[:, 0, MID_AT:MID_AT + P], mid[0][:, :], ident[:, :])\
                    .then_inc(tr_mid[0].sem, 1)

            def b_keys(b):
                pe.wait_ge(ctxb_in.sem, ctxb_in.after(b))
                pe.wait_ge(x2_out.sem, x2_out.after(b))
                project(pb, 0, ctx_b, w_att[:, 1, :]).then_inc(mm_k.sem, 1)

            def b_values(b):
                pe.wait_ge(kl_out.sem, kl_out.after(b))
                project(pb, 0, ctx_b, w_att[:, 2, :]).then_inc(mm_v.sem, 1)

            def b_queries(b):
                pe.wait_ge(ln_out[2].sem, ln_out[2].after(b))
                pe.wait_ge(vl_out.sem, vl_out.after(b))
                project(pb, 0, xn_b, w_att[:, 0, :]).then_inc(mm_qq.sem, 1)

            q_halves = words(q_diag[:, :, :])

            def c_scores(b, g):
                if g == 0:
                    pe.wait_ge(qd_out.sem, qd_out.after(b))
                    if not first(b):
                        pe.wait_ge(x4_out.sem, x4_out.after(b - 1))
                else:
                    pe.wait_ge(sc_in.sem, sc_in.after(b, g))
                mm(pc[:, 0, :], ident_bf[:, :], band_bf[:, :, :].rearrange("p n k -> p (n k)"),
                   start=True, stop=False)
                for i in range(GB):
                    blk = g * GB + i
                    place = pc[:, 0, i * KEYS:(i + 1) * KEYS]
                    keys = slice(blk * QB, blk * QB + KEYS)
                    mm(place, q_halves[:, blk, :, HI], k_h[:, keys], start=False, stop=False)
                    mm(place, q_halves[:, blk, :, HI], k_l[:, keys], start=False, stop=False)
                    last = mm(place, q_halves[:, blk, :, LO], k_h[:, keys], start=False, stop=(i == GB - 1))
                last.then_inc(mm_sc.sem, 1)

            p_halves = words(sc_t[:, :, :, :])
            v_halves = words(v_diag[:, :, :, :].rearrange("p n a c -> p n (a c)"))

            def c_attend(b, g):
                pe.wait_ge(pt_out.sem, pt_out.after(b, g + 1))
                if g == 0:
                    pe.wait_ge(vd_out.sem, vd_out.after(b))
                    if not first(b):
                        pe.wait_ge(x4_out.sem, x4_out.after(b - 1))
                else:
                    pe.wait_ge(av_out.sem, av_out.after(b, 2 * g))
                for i in range(GB):
                    blk = g * GB + i
                    place = pc[:, 1, i * KEYS:(i + 1) * KEYS]
                    for m, (v_part, p_part) in enumerate(((HI, HI), (HI, LO), (LO, HI))):
                        last = mm(place, v_halves[:, blk, :, v_part], p_halves[:, g % 2, i, :, p_part],
                                  start=(m == 0), stop=(m == 2))
                last.then_inc(mm_av.sem, 1)

            def c_output(b):
                pe.wait_ge(av_out.sem, av_out.after(b))
                pe.wait_ge(sc_in.sem, sc_in.after(b))
                project(pc, 0, at, w_att[:, 3, :]).then_inc(mm_o.sem, 1)

            def c_router(b):
                pe.wait_ge(xt_out[1].sem, xt_out[1].after(b))
                for j in range(KT):
                    last = mm(pc[:, 0, 0:E1 + E1 * RANK], xt_c[:, j * P:(j + 1) * P], w_ra1[:, j, :],
                              start=(j == 0), stop=(j == KT - 1))
                last.then_inc(mm_ra[1].sem, 1)

            def c_mid(b):
                pe.wait_ge(mid_out[1].sem, mid_out[1].after(b))
                nc.tensor.transpose(pc[:, 0, 384:384 + P], ident[:, :], ident[:, :])
                nc.tensor.transpose(pc[0:E1 * RANK, 0, MID_AT:MID_AT + P], mid[1][:, :], ident[:, :])\
                    .then_inc(tr_mid[1].sem, 1)

            def c_delta(b):
                pe.wait_ge(midt_out[1].sem, midt_out[1].after(b))
                for h in range(2):
                    last = mm(pc[:, h, :], mid_t[1][:, :], w_b1[:, h * HALF:(h + 1) * HALF],
                              start=True, stop=True)
                last.then_inc(mm_ffn[1].sem, 1)

            def step(i, do_a, do_b, do_c):
                b, c = i - 1, i - 2
                if do_c:
                    c_scores(c, 0)
                if do_a:
                    a_context(i)
                if do_b:
                    rows_to_features(b, 0, 1, xn_b, pb)
                if do_c:
                    c_scores(c, 1)
                if do_b:
                    b_router(b)
                if do_a:
                    a_query(i)
                if do_b:
                    b_base(b, 1)
                if do_c:
                    c_attend(c, 0)
                    c_scores(c, 2)
                if do_b:
                    b_mid(b)
                if do_a:
                    a_corr(i)
                if do_c:
                    c_attend(c, 1)
                    c_scores(c, 3)
                if do_b:
                    b_base(b, 0)
                    b_base_end(b)
                if do_c:
                    c_attend(c, 2)
                    c_attend(c, 3)
                    c_output(c)
                if do_b:
                    b_keys(b)
                    b_values(b)
                if do_a:
                    a_weights(i)
                if do_b:
                    b_queries(b)
                if do_c:
                    rows_to_features(c, 1, 3, xn_c, pc)
                    c_router(c)
                if do_a:
                    a_odd(i)
                if do_c:
                    c_mid(c)
                    c_delta(c)
                if do_a:
                    a_aggregate(i)

            pe.wait_ge(tab_in.sem, TABLES_IN)
            step(0, True, False, False)
            pe.wait_ge(const_in.sem, CONSTS_IN)
            pe.wait_ge(const_set.sem, CONSTS_SET)
            pe.wait_ge(w_lo.sem, WEIGHTS_SPLIT)
            step(1, True, True, False)
            step(2, True, True, True)
            with pe.Fori(3, BATCH) as i:
                step(i, True, True, True)
            step(BATCH, False, True, True)
            step(BATCH + 1, False, False, True)

        @block.scalar
        def _(act):
            def copy(dst, src):
                return nc.scalar.activation(dst, src, ACT.Copy)

            def a_values(b):
                act.wait_ge(mm_vb.sem, mm_vb.after(b))
                if not first(b):
                    act.wait_ge(mm_agg.sem, mm_agg.after(b - 1))
                copy(v_b[:, :], pa_lo).then_inc(vb_out.sem, 1)
                act.wait_ge(mm_vc.sem, mm_vc.after(b))
                copy(v_c[:, :], pa_hi).then_inc(vc_out.sem, 1)

            def a_query(b):
                act.wait_ge(mm_q.sem, mm_q.after(b))
                copy(q_spec[:, :], pa_lo).then_inc(q_out.sem, 1)

            def a_exp(b):
                for j in range(KT):
                    if j % 4 == 0:
                        act.wait_ge(negmax_out.sem, negmax_out.after(b, j // 4 + 1))
                    nc.scalar.activation(prob[:, j, :], pa[:, j // 4, (j % 4) * P:(j % 4 + 1) * P], ACT.Exp,
                                         bias=neg_max[:, j:j + 1]).then_inc(exp_out.sem, 1)

            def a_weights(b):
                for h in range(2):
                    act.wait_ge(tr_w.sem, tr_w.after(b, h + 1))
                    copy(wt[:, h * HALF:(h + 1) * HALF], pa[:, 2 + h, :]).then_inc(wt_out.sem, 1)
                act.wait_ge(mm_wo.sem, mm_wo.after(b))
                copy(w_odd[:, :], pa_hi).then_inc(wo_out.sem, 1)

            def b_features(b):
                for h in range(2):
                    act.wait_ge(tr_x[0].sem, tr_x[0].after(b, h + 1))
                    copy(xt_h[:, h * HALF:(h + 1) * HALF], pb[:, h, :]).then_inc(xt_out[0].sem, 1)

            def b_keys(b):
                act.wait_ge(mm_k.sem, mm_k.after(b))
                if not first(b):
                    act.wait_ge(mm_sc.sem, mm_sc.after(b - 1))
                nc.scalar.activation(k_h[:, PAD:PAD + D], pb_all, ACT.Identity, bias=bias_att[:, 1:2])\
                    .then_inc(kh_out.sem, 1)

            v_halves = words(v_pad[:, :])

            def b_values(b):
                act.wait_ge(mm_v.sem, mm_v.after(b))
                nc.scalar.activation(v_halves[:, PAD:PAD + D, HI], pb_all, ACT.Identity,
                                     bias=bias_att[:, 2:3]).then_inc(vh_out.sem, 1)

            def b_value_blocks(b, odd):
                act.wait_ge(vt_out.sem, vt_out.after(b, odd + 1))
                if odd == 0:
                    act.wait_ge(diag_set.sem, 2)
                    if not first(b):
                        act.wait_ge(mm_av.sem, mm_av.after(b - 1))
                for pair in range(4):
                    rows = slice(32 * pair, 32 * pair + 32)
                    place = v_diag[rows, :, :, pair * HD:(pair + 1) * HD]\
                        .rearrange("p (m o) a d -> p o m a d", o=2)[:, odd]
                    copy(place, v_t[odd][rows, :].rearrange("p (m a d) -> p m a d", a=2, d=HD))\
                        .then_inc(vd_out.sem, 1)

            def b_queries(b):
                act.wait_ge(mm_qq.sem, mm_qq.after(b))
                act.wait_ge(pl_out.sem, pl_out.after(b - 1)) if not first(b) else None
                nc.scalar.activation(words(q_hl)[:, :, HI], pb_all, ACT.Identity, bias=bias_att[:, 0:1])\
                    .then_inc(qh_out.sem, 1)

            def b_query_blocks(b, pair):
                if pair == 0:
                    act.wait_ge(ql_out.sem, ql_out.after(b))
                    act.wait_ge(diag_set.sem, 2)
                    if not first(b):
                        act.wait_ge(mm_sc.sem, mm_sc.after(b - 1))
                rows = slice(32 * pair, 32 * pair + 32)
                source = q_hl[rows, :].rearrange("p (n t) -> p n t", t=QB)
                for a in range(2):
                    col = (2 * pair + a) * QB
                    nc.scalar.activation(q_diag[rows, :, col:col + QB], source, ACT.Copy,
                                         scale=par[rows, a:a + 1]).then_inc(qd_out.sem, 1)

            def experts_exp(b, n, experts):
                act.wait_ge(gt[n].sem, gt[n].after(b, 5))
                nc.scalar.activation(lg_exp[n][:, 0:experts], lg[n][:, 0:experts], ACT.Exp,
                                     bias=lg_neg[n][:, :]).then_inc(gt_exp[n].sem, 1)

            def experts_mid(b, n, source, rows):
                act.wait_ge(tr_mid[n].sem, tr_mid[n].after(b))
                copy(mid_t[n][:, :], source[0:rows, 0, MID_AT:MID_AT + P]).then_inc(midt_out[n].sem, 1)

            def c_exp(b, g):
                act.wait_ge(sc_in.sem, sc_in.after(b, g + 1))
                nc.scalar.activation(sc[:, g % 2, :, :], sc[:, g % 2, :, :], ACT.Exp, scale=ATT_SCALE)\
                    .then_inc(sc_exp.sem, 1)

            def c_high(b, g):
                act.wait_ge(p_out.sem, p_out.after(b, g + 1))
                copy(words(p_hl[:, g % 2, :, :])[:, :, :, HI], sc[:, g % 2, :, :]).then_inc(ph_out.sem, 1)

            def c_attended(b, g):
                act.wait_ge(mm_av.sem, mm_av.after(b, g + 1))
                if g == 0 and not first(b):
                    act.wait_ge(out_done.sem, out_done.after(b - 1))
                for a in range(2):
                    rows = slice(64 * a, 64 * a + 64)
                    copy(at[rows, g * GW:(g + 1) * GW].rearrange("p (n t) -> p n t", t=QB),
                         pc[rows, 1, :].rearrange("p (n s) -> p n s", s=KEYS)[:, :, a * QB:(a + 1) * QB])\
                        .then_inc(av_out.sem, 1)

            def c_features(b):
                for h in range(2):
                    act.wait_ge(tr_x[1].sem, tr_x[1].after(b, h + 1))
                    copy(xt_c[:, h * HALF:(h + 1) * HALF], pc[:, h, :]).then_inc(xt_out[1].sem, 1)

            def step(i, do_a, do_b, do_c):
                b, c = i - 1, i - 2
                if do_c:
                    c_exp(c, 0)
                if do_a:
                    a_values(i)
                if do_b:
                    b_features(b)
                if do_c:
                    c_exp(c, 1)
                    c_high(c, 0)
                if do_a:
                    a_query(i)
                if do_b:
                    experts_exp(b, 0, E0)
                    experts_mid(b, 0, pb, P)
                if do_c:
                    c_attended(c, 0)
                    c_high(c, 1)
                    c_exp(c, 2)
                    c_attended(c, 1)
                if do_a:
                    a_exp(i)
                if do_c:
                    c_exp(c, 3)
                    c_high(c, 2)
                    c_attended(c, 2)
                    c_high(c, 3)
                    c_attended(c, 3)
                if do_b:
                    b_keys(b)
                    b_values(b)
                if do_a:
                    a_weights(i)
                if do_b:
                    b_value_blocks(b, 0)
                if do_c:
                    c_features(c)
                if do_b:
                    b_value_blocks(b, 1)
                    b_queries(b)
                if do_c:
                    experts_exp(c, 1, E1)
                if do_b:
                    b_query_blocks(b, 0)
                if do_c:
                    experts_mid(c, 1, pc, E1 * RANK)
                if do_b:
                    for pair in range(1, 4):
                        b_query_blocks(b, pair)

            act.wait_ge(tab_in.sem, TABLES_IN)
            act.wait_ge(const_set.sem, CONSTS_SET)
            step(0, True, False, False)
            act.wait_ge(w_in.sem, 32)
            for part, whole in ((w_base_h, base_f32), (w_ra0_h, ra0_f32)):
                nc.scalar.activation(part[:, :, :].rearrange("p k n -> p (k n)"), whole, ACT.Copy,
                                     scale=W_SCALE).then_inc(w_hi.sem, 1)
            act.wait_ge(const_in.sem, CONSTS_IN)
            step(1, True, True, False)
            step(2, True, True, True)
            with act.Fori(3, BATCH) as i:
                step(i, True, True, True)
            step(BATCH, False, True, True)
            step(BATCH + 1, False, False, True)

        @block.vector
        def _(dve):
            v = nc.vector

            def layer_norm(b, n, rows, place):
                for h in range(2):
                    v.bn_stats(bn[n][:, h, :], rows[:, h * HALF:(h + 1) * HALF]).then_inc(ln_bn[n].sem, 1)
                dve_wait(dve, ln_bn[n], ln_bn[n].after(b))
                v.bn_aggr(mv[n][:, :], bn[n][:, :, :]).then_inc(ln_mv[n].sem, 1)
                var, t, u, y, steps = rs_v[n], rs_t[n], rs_u[n], rs_y[n], ln_rs[n]
                dve.wait_ge(ln_mv[n].sem, ln_mv[n].after(b))
                v.tensor_scalar(var[:, :], mv[n][:, 1:2], 1e-5, None, ALU.add).then_inc(steps.sem, 1)
                dve.wait_ge(steps.sem, steps.after(b, 1))
                v.tensor_scalar(y[:, :].bitcast(I32), var[:, :].bitcast(I32), -0.5, float(RSQRT_MAGIC),
                                ALU.mult, ALU.add).then_inc(steps.sem, 1)
                for k in range(RSQRT_ROUNDS):
                    at_step = 2 + 4 * k
                    dve.wait_ge(steps.sem, steps.after(b, at_step))
                    v.scalar_tensor_tensor(out=t[:, :], in0=y[:, :], scalar=y[:, :], in1=var[:, :],
                                           op0=ALU.mult, op1=ALU.mult).then_inc(steps.sem, 1)
                    dve.wait_ge(steps.sem, steps.after(b, at_step + 1))
                    v.tensor_scalar(u[:, :], t[:, :], 0.375, -1.25, ALU.mult, ALU.add).then_inc(steps.sem, 1)
                    dve.wait_ge(steps.sem, steps.after(b, at_step + 2))
                    v.tensor_scalar(u[:, :], u[:, :], t[:, :], 1.875, ALU.mult, ALU.add)\
                        .then_inc(steps.sem, 1)
                    dve.wait_ge(steps.sem, steps.after(b, at_step + 3))
                    v.tensor_tensor(y[:, :], y[:, :], u[:, :], ALU.mult).then_inc(steps.sem, 1)
                dve.wait_ge(steps.sem, steps.after(b))
                v.tensor_scalar(place[:, :], rows[:, :], mv[n][:, 0:1], y[:, :],
                                ALU.subtract, ALU.mult).then_inc(ln_out[n].sem, 1)

            def a_norm(b):
                dve.wait_ge(x_in.sem, x_in.after(b))
                if not first(b):
                    dve.wait_ge(mm_we.sem, mm_we.after(b - 1))
                layer_norm(b, 0, x_a, xn_a)

            def a_products(b):
                dve.wait_ge(q_out.sem, q_out.after(b))
                dve.wait_ge(vc_out.sem, vc_out.after(b))
                v.tensor_tensor(c2, q_spec[:, :], v_c[:, :], ALU.mult).then_inc(prod_q.sem, 1)
                v.tensor_tensor(c1[:, :], q_spec[:, :], v_b[:, :], ALU.mult).then_inc(prod_q.sem, 1)

            def a_top(b):
                for h in range(2):
                    dve_wait(dve, mm_corr, mm_corr.after(b, h + 1))
                    for j in range(4 * h, 4 * h + 4):
                        v.max(top8[:, j, :], pa[:, h, (j % 4) * P:(j % 4 + 1) * P]).then_inc(top_found.sem, 1)
                    dve_wait(dve, top_found, top_found.after(b, 4 * h + 4))
                    for j in range(4 * h, 4 * h + 4):
                        v.match_replace(rest[:, j, :], top8[:, j, :], pa[:, h, (j % 4) * P:(j % 4 + 1) * P],
                                        GONE).then_inc(top_gone.sem, 1)
                    dve.wait_ge(top_gone.sem, top_gone.after(b, 4 * h + 4))
                    v.tensor_scalar(neg_max[:, 4 * h:4 * h + 4], top8[:, 4 * h:4 * h + 4, 0], -1.0, None,
                                    ALU.mult).then_inc(negmax_out.sem, 1)

            def a_ninth(b):
                v.tensor_reduce(ninth[:, :, 0], rest[:, :, :], AX_X, ALU.max).then_inc(ninth_found.sem, 1)
                dve_wait(dve, ninth_found, ninth_found.after(b))
                for j in range(KT):
                    v.match_replace(rest[:, j, :], ninth[:, j, :], rest[:, j, :], GONE)\
                        .then_inc(ninth_gone.sem, 1)
                dve.wait_ge(exp_out.sem, exp_out.after(b))
                for j in range(KT):
                    dve.wait_ge(ninth_gone.sem, ninth_gone.after(b, j + 1))
                    v.scalar_tensor_tensor(out=prob[:, j, :], in0=rest[:, j, :], scalar=GONE_MAX,
                                           in1=prob[:, j, :], op0=ALU.is_le, op1=ALU.mult,
                                           accum_out=psum_w[:, j:j + 1]).then_inc(prob_masked.sem, 1)
                dve.wait_ge(prob_masked.sem, prob_masked.after(b))
                v.reciprocal(rec_w[:, :], psum_w[:, :]).then_inc(rec_out.sem, 1)
                dve.wait_ge(rec_out.sem, rec_out.after(b))
                v.tensor_tensor(prob[:, :, :], prob[:, :, :],
                                rec_w[:, :].unsqueeze(2).to_broadcast([P, KT, P]), ALU.mult)\
                    .then_inc(prob_out.sem, 1)

            def a_products_even(b):
                dve.wait_ge(mm_we.sem, mm_we.after(b))
                v.tensor_tensor(p1[:, :], pa_lo, v_b[:, :], ALU.mult).then_inc(prod_e.sem, 1)
                v.tensor_tensor(p2[:, :], pa_lo, v_c[:, :], ALU.mult).then_inc(prod_e.sem, 1)

            def a_products_odd(b):
                dve.wait_ge(mm_bo.sem, mm_bo.after(b))
                dve.wait_ge(wo_out.sem, wo_out.after(b))
                v.tensor_tensor(p3, pa_hi, w_odd[:, :], ALU.mult).then_inc(prod_o.sem, 1)
                dve.wait_ge(mm_co.sem, mm_co.after(b))
                v.tensor_tensor(p4, pa_lo, w_odd[:, :], ALU.mult).then_inc(prod_o.sem, 1)

            def a_residual(b):
                dve.wait_ge(mm_agg.sem, mm_agg.after(b))
                if not first(b):
                    dve.wait_ge(x2_moved.sem, x2_moved.after(b - 1))
                v.tensor_tensor(x_b[:, :], pa_hi, x_a[:, :], ALU.add).then_inc(x1_out.sem, 1)

            def b_norm(b, n, before):
                dve.wait_ge(before.sem, before.after(b))
                if n == 1:
                    if not first(b):
                        dve.wait_ge(mm_qq.sem, mm_qq.after(b - 1))
                else:
                    dve.wait_ge(tr_x[0].sem, tr_x[0].after(b))
                layer_norm(b, n, x_b, xn_b)

            def b_features(b):
                for h in range(2):
                    cols = slice(h * HALF, (h + 1) * HALF)
                    dve.wait_ge(xt_out[0].sem, xt_out[0].after(b, h + 1))
                    v.tensor_tensor(xt_l[:, cols], pb[:, h, :], xt_h[:, cols], ALU.subtract)\
                        .then_inc(xtl_out.sem, 1)

            def b_base(b):
                dve.wait_ge(mm_ffn[0].sem, mm_ffn[0].after(b))
                dve.wait_ge(bias_added.sem, bias_added.after(b))
                v.scalar_tensor_tensor(out=x_b[:, :], in0=pb_all, scalar=1.0 / W_SCALE, in1=x_b[:, :],
                                       op0=ALU.mult, op1=ALU.add).then_inc(x2_out.sem, 1)

            v_halves = words(v_pad[:, :])

            def low_half(place, column, high, signal):
                v.scalar_tensor_tensor(out=place, in0=pb_all, scalar=bias_att[:, column:column + 1], in1=high,
                                       op0=ALU.add, op1=ALU.subtract).then_inc(signal.sem, 1)

            def b_keys(b):
                dve.wait_ge(kh_out.sem, kh_out.after(b))
                low_half(k_l[:, PAD:PAD + D], 1, k_h[:, PAD:PAD + D], kl_out)

            def b_values(b):
                dve.wait_ge(vh_out.sem, vh_out.after(b))
                low_half(v_halves[:, PAD:PAD + D, LO], 2, v_halves[:, PAD:PAD + D, HI], vl_out)
                dve.wait_ge(vl_out.sem, vl_out.after(b))
                dve.wait_ge(mm_ffn[0].sem, mm_ffn[0].after(b))
                for odd in range(2):
                    v.transpose(v_t[odd], v_pad[:, odd * QB:odd * QB + D]).then_inc(vt_out.sem, 1)

            def b_queries(b):
                dve.wait_ge(qh_out.sem, qh_out.after(b))
                low_half(words(q_hl)[:, :, LO], 0, words(q_hl)[:, :, HI], ql_out)

            def gates(b, n, source, experts, scale):
                g = gt[n]
                width = experts * RANK
                logit_scale = [1.0 / W_SCALE, 1.0][n]
                dve.wait_ge(mm_ra[n].sem, mm_ra[n].after(b))
                v.tensor_scalar(lg[n][:, 0:experts], source[:, 0, 0:experts], logit_scale, None, ALU.mult)\
                    .then_inc(g.sem, 1)
                dve_wait(dve, g, g.after(b, 1))
                v.max(lg_top[n][:, :], lg[n][:, 0:8]).then_inc(g.sem, 1)
                dve.wait_ge(g.sem, g.after(b, 2))
                v.tensor_copy(lg_pick[n][:, 0:2], lg_top[n][:, 0:2]).then_inc(g.sem, 1)
                dve_wait(dve, g, g.after(b, 3))
                v.match_replace(lg_mark[n][:, :], lg_pick[n][:, :], lg[n][:, :], TAKEN).then_inc(g.sem, 1)
                v.tensor_scalar(lg_neg[n][:, :], lg_top[n][:, 0:1], -1.0, None, ALU.mult).then_inc(g.sem, 1)
                dve.wait_ge(g.sem, g.after(b, 5))
                dve.wait_ge(gt_exp[n].sem, gt_exp[n].after(b))
                v.scalar_tensor_tensor(out=gate[n][:, 0:experts], in0=lg_mark[n][:, 0:experts],
                                       scalar=TAKEN_MIN, in1=lg_exp[n][:, 0:experts], op0=ALU.is_ge,
                                       op1=ALU.mult, accum_out=gate_sum[n][:, :]).then_inc(g.sem, 1)
                dve.wait_ge(g.sem, g.after(b, 6))
                v.reciprocal(gate_rec[n][:, :], gate_sum[n][:, :]).then_inc(g.sem, 1)
                dve.wait_ge(g.sem, g.after(b, 7))
                v.tensor_scalar(gate[n][:, 0:experts], gate[n][:, 0:experts], gate_rec[n][:, :], scale,
                                ALU.mult, ALU.mult).then_inc(g.sem, 1)
                dve.wait_ge(g.sem, g.after(b, 8))
                v.tensor_tensor(mid[n][:, :].rearrange("p (e r) -> p e r", r=RANK),
                                source[:, 0, experts:experts + width].rearrange("p (e r) -> p e r", r=RANK),
                                gate[n][:, 0:experts].unsqueeze(2).to_broadcast([P, experts, RANK]),
                                ALU.mult).then_inc(mid_out[n].sem, 1)

            def c_scores(b, g):
                source = pc[:, 0, :].rearrange("p (n k) -> p n k", k=KEYS)
                blocks = slice(g * GB, (g + 1) * GB)
                dve.wait_ge(mm_sc.sem, mm_sc.after(b, g + 1))
                v.tensor_reduce(sc_max[:, blocks], source, AX_X, ALU.max).then_inc(max_out.sem, 1)
                dve.wait_ge(max_out.sem, max_out.after(b, g + 1))
                v.tensor_tensor(sc[:, g % 2, :, :], source,
                                sc_max[:, blocks].unsqueeze(2).to_broadcast([P, GB, KEYS]),
                                ALU.subtract).then_inc(sc_in.sem, 1)

            def c_sums(b, g):
                blocks = slice(g * GB, (g + 1) * GB)
                dve.wait_ge(sc_exp.sem, sc_exp.after(b, g + 1))
                v.tensor_reduce(sc_sum[:, blocks], sc[:, g % 2, :, :], AX_X, ALU.add).then_inc(sum_out.sem, 1)
                dve.wait_ge(sum_out.sem, sum_out.after(b, g + 1))
                v.reciprocal(sc_rec[:, blocks], sc_sum[:, blocks]).then_inc(srec_out.sem, 1)

            def c_transpose(b, g):
                part = words(p_hl[:, g % 2, :, :])
                dve.wait_ge(ph_out.sem, ph_out.after(b, g + 1))
                v.tensor_tensor(part[:, :, :, LO], sc[:, g % 2, :, :], part[:, :, :, HI], ALU.subtract)\
                    .then_inc(pl_out.sem, 1)
                dve.wait_ge(pl_out.sem, pl_out.after(b, g + 1))
                if g >= 2:
                    dve.wait_ge(mm_av.sem, mm_av.after(b, g - 1))
                v.transpose(sc_t[:, g % 2, :, :].rearrange("p n k -> p (n k)"),
                            p_hl[:, g % 2, :, :].rearrange("p n k -> p (n k)")).then_inc(pt_out.sem, 1)

            def c_attention_residual(b):
                dve.wait_ge(mm_o.sem, mm_o.after(b))
                dve.wait_ge(x2_moved.sem, x2_moved.after(b))
                v.scalar_tensor_tensor(out=x_c[:, :], in0=pc_all, scalar=bias_att[:, 3:4], in1=x_c[:, :],
                                       op0=ALU.add, op1=ALU.add).then_inc(x3_out.sem, 1)

            def c_norm(b):
                dve.wait_ge(x3_out.sem, x3_out.after(b))
                layer_norm(b, 3, x_c, xn_c)

            def c_result(b):
                dve.wait_ge(mm_ffn[1].sem, mm_ffn[1].after(b))
                v.tensor_tensor(xn_c[:, :], pc_all, x_c[:, :], ALU.add).then_inc(x4_out.sem, 1)

            def step(i, do_a, do_b, do_c):
                b, c = i - 1, i - 2
                if do_b:
                    b_norm(b, 1, x1_out)
                if do_c:
                    c_scores(c, 0)
                if do_a:
                    a_norm(i)
                if do_c:
                    c_sums(c, 0)
                if do_b:
                    b_features(b)
                if do_c:
                    c_scores(c, 1)
                    c_transpose(c, 0)
                if do_a:
                    a_products(i)
                if do_c:
                    c_sums(c, 1)
                if do_b:
                    gates(b, 0, pb, E0, SCALE0)
                if do_c:
                    c_scores(c, 2)
                    c_transpose(c, 1)
                if do_a:
                    a_top(i)
                if do_c:
                    c_sums(c, 2)
                    c_scores(c, 3)
                if do_a:
                    a_ninth(i)
                if do_c:
                    c_transpose(c, 2)
                    c_sums(c, 3)
                if do_b:
                    b_base(b)
                if do_c:
                    c_transpose(c, 3)
                if do_b:
                    b_norm(b, 2, x2_out)
                    b_keys(b)
                if do_c:
                    c_attention_residual(c)
                if do_b:
                    b_values(b)
                if do_c:
                    c_norm(c)
                if do_b:
                    b_queries(b)
                if do_a:
                    a_products_even(i)
                    a_products_odd(i)
                if do_c:
                    gates(c, 1, pc, E1, SCALE1)
                    c_result(c)
                if do_a:
                    a_residual(i)

            v.memset(ninth[:, :, :], GONE).then_inc(const_set.sem, 1)
            v.memset(lg[0][:, :], GONE).then_inc(const_set.sem, 1)
            v.memset(lg[1][:, :], GONE).then_inc(const_set.sem, 1)
            v.memset(lg_pick[0][:, :], GONE).then_inc(const_set.sem, 1)
            v.memset(lg_pick[1][:, :], GONE).then_inc(const_set.sem, 1)
            v.memset(k_h[:, :], 0.0).then_inc(const_set.sem, 1)
            v.memset(k_l[:, :], 0.0).then_inc(const_set.sem, 1)
            v.memset(v_pad[:, :], 0.0).then_inc(const_set.sem, 1)
            dve.wait_ge(tab_in.sem, TABLES_IN)
            v.tensor_copy(ident_bf[:, :], ident[:, :])
            v.tensor_copy(band_bf[:, :, :], band_mask[:, :].unsqueeze(1).to_broadcast([P, GB, KEYS]))\
                .then_inc(const_set.sem, 1)
            dve.wait_ge(const_set.sem, CONSTS_SET)
            step(0, True, False, False)
            for n, (part, high, whole) in enumerate(((w_base_l, w_base_h, base_f32), (w_ra0_l, w_ra0_h, ra0_f32))):
                dve.wait_ge(w_hi.sem, n + 1)
                v.scalar_tensor_tensor(out=part[:, :, :].rearrange("p k n -> p (k n)"), in0=whole,
                                       scalar=W_SCALE, in1=high[:, :, :].rearrange("p k n -> p (k n)"),
                                       op0=ALU.mult, op1=ALU.subtract).then_inc(w_lo.sem, 1)
            dve.wait_ge(const_in.sem, CONSTS_IN)
            step(1, True, True, False)
            step(2, True, True, True)
            with dve.Fori(3, BATCH) as i:
                step(i, True, True, True)
            step(BATCH, False, True, True)
            step(BATCH + 1, False, False, True)

        @block.gpsimd
        def _(pool):
            g_ = nc.gpsimd

            def b_bias(b):
                pool.wait_ge(ln_out[1].sem, ln_out[1].after(b))
                g_.tensor_tensor(x_b[:, :], x_b[:, :], bias_base[:, :], ALU.add).then_inc(bias_added.sem, 1)

            def b_move(b):
                pool.wait_ge(x2_out.sem, x2_out.after(b))
                if not first(b):
                    pool.wait_ge(x4_out.sem, x4_out.after(b - 1))
                g_.tensor_tensor(idle_pool[:, :], ident[:, 0:1], ident[:, 0:1], ALU.add)
                g_.tensor_copy(x_c[:, :], x_b[:, :]).then_inc(x2_moved.sem, 1)

            def c_normalise(b, g):
                blocks = slice(g * GB, (g + 1) * GB)
                pool.wait_ge(srec_out.sem, srec_out.after(b, g + 1))
                g_.tensor_tensor(sc[:, g % 2, :, :], sc[:, g % 2, :, :],
                                 sc_rec[:, blocks].unsqueeze(2).to_broadcast([P, GB, KEYS]), ALU.mult)\
                    .then_inc(p_out.sem, 1)

            def step(i, do_b, do_c):
                b, c = i - 1, i - 2
                if do_b:
                    b_bias(b)
                if do_c:
                    for g in range(NG):
                        c_normalise(c, g)
                if do_b:
                    b_move(b)

            pool.wait_ge(w_lo.sem, WEIGHTS_SPLIT)
            g_.memset(v_diag[:, :, :, :], 0.0).then_inc(diag_set.sem, 1)
            g_.memset(q_diag[:, :, :], 0.0).then_inc(diag_set.sem, 1)
            step(1, True, False)
            step(2, True, True)
            with pool.Fori(3, BATCH) as i:
                step(i, True, True)
            step(BATCH, True, True)
            step(BATCH + 1, False, True)


_OUTS = [((32, 128, 1024), "float32")]


def kernel(**inputs):
    import concourse.bacc as bacc
    from concourse.bass_utils import run_bass_kernel_spmd as run

    f = {k: np.asarray(v) for k, v in inputs.items()}

    def tiles(w):
        return w.T.reshape(8, 128, -1).transpose(1, 0, 2)

    head_order = [2 * pair + a for a in range(2) for pair in range(4)]
    channels = np.concatenate([np.arange(16 * h, 16 * h + 16) for h in head_order])
    key = np.arange(32)[None, :] - (np.arange(128) % 16)[:, None]
    odd_head = (np.arange(128) // 16) % 2
    data = {
        "x": f["x"],
        "ctx_in": f["ctx_4096"],
        "spectra": spectral_tables(),
        "identity": np.eye(128, dtype=np.float32),
        "band": np.where((key >= 0) & (key < 16), 0.0, GONE).astype(np.float32),
        "parity": np.stack([1 - odd_head, odd_head], 1).astype(np.float32),
        "base_w": tiles(f["L0_ffn_W_base"]),
        "base_b": f["L0_ffn_b_base"],
        "ra0": tiles(np.concatenate([f["L0_ffn_W_router"], f["L0_ffn_A_stack"].reshape(128, 1024)])),
        "b0": f["L0_ffn_B_stack"].transpose(0, 2, 1).reshape(128, 1024),
        "wqkvo": np.stack([f["L1_xattn_Wq"].T, f["L1_xattn_Wk"].T, f["L1_xattn_Wv"].T,
                           f["L1_xattn_Wo"].T[channels]], 1),
        "biases": np.stack([f["L1_xattn_bq"], f["L1_xattn_bk"], f["L1_xattn_bv"], f["L1_xattn_bo"]], 1),
        "ra1": tiles(np.concatenate([f["L1_ffn_Wr"], f["L1_ffn_A"].reshape(64, 1024)])),
        "b1": f["L1_ffn_B"].transpose(0, 2, 1).reshape(64, 1024),
    }
    nc = bacc.Bacc("TRN2", target_bir_lowering=False, num_devices=1)
    arrays, args = {}, []
    for name, a in data.items():
        a = np.ascontiguousarray(a)
        arrays[f"in_{name}"] = a
        args.append(nc.dram_tensor(f"in_{name}", a.shape, mybir.dt.from_np(a.dtype), kind="ExternalInput").ap())
    shape, dtype = _OUTS[0]
    args.append(nc.dram_tensor("out_0", shape, mybir.dt.from_np(np.dtype(dtype)), kind="ExternalOutput").ap())
    build(nc, *args)
    r = run(nc, [arrays], core_ids=[0])
    return r.results[0]["out_0"]
```

```python
import math
from contextlib import ExitStack

import numpy as np

import concourse.bass as bass
from concourse import mybir

F32 = mybir.dt.float32
I32 = mybir.dt.int32
F16 = mybir.dt.float16
BF16 = mybir.dt.bfloat16
ALU = mybir.AluOpType
ACT = mybir.ActivationFunctionType
AX_X = mybir.AxisListType.X

P = 128
GONE = -3.0e38
GONE_MAX = -2.9e38
TAKEN = 3.0e38
TAKEN_MIN = 2.9e38
RSQRT_MAGIC = 0x5F3759DF - 2 ** 31
RSQRT_K = 8.0 / 3.0
RSQRT_STEPS = 7
W_SCALE = 256.0


class Signal:

    def __init__(self, sem, per):
        self.sem = sem
        self.per = per

    def after(self, b, k=None):
        return b * self.per + (self.per if k is None else k)


def spectral_tables():
    n = P
    half = n // 2
    t = np.arange(n, dtype=np.float64)
    k = np.arange(half, dtype=np.float64)
    angle = 2.0 * np.pi * np.outer(t, k) / n
    alt = (-1.0) ** t

    fwd = np.concatenate([np.cos(angle), -np.sin(angle)], 1)
    fwd[:, half] = alt
    scale = np.full((half, 1), 2.0 / n)
    scale[0] = 1.0 / n
    cos, sin = scale * np.cos(angle).T, scale * np.sin(angle).T
    corr_1 = np.concatenate([cos, -sin])
    corr_2 = np.concatenate([sin, cos])
    corr_1[half] = 0.0
    corr_2[0] = 0.0
    corr_2[half] = alt / n

    angle = 2.0 * np.pi * np.outer(np.arange(2 * n), t + 0.5) / (2 * n)
    weights_re, weights_im = np.cos(angle[:n]), -np.sin(angle[:n])
    ctx_re, ctx_im = np.cos(angle), -np.sin(angle)
    ctx_re, ctx_im = (np.concatenate([m[:n - 1], m[n - 1:].sum(0, keepdims=True)]) for m in (ctx_re, ctx_im))
    agg_re, agg_im = np.cos(angle[:n]).T / n, -np.sin(angle[:n]).T / n
    tables = [fwd, corr_1, corr_2, ctx_re, ctx_im, weights_re, weights_im, agg_re, agg_im]
    return np.stack([m.astype(np.float32) for m in tables], 1)


(FWD, CORR_1, CORR_2, CTX_RE, CTX_IM, WEIGHTS_RE, WEIGHTS_IM, AGG_RE, AGG_IM) = range(9)


def first(b):
    return isinstance(b, int) and b == 0


def words(t):
    v = t.bitcast(F16)
    names = " ".join("abc"[:len(v.shape) - 1])
    return v.rearrange(f"{names} (n two) -> {names} n two", two=2)


LO, HI = 0, 1


def build(nc, x, ctx_in, spectra, identity, band, parity, base_w, base_b, ra0, b0, wqkvo, biases,
          ra1, b1, out):
    BATCH, _, D = x.shape
    KT = D // P
    HALF = D // 2
    E0, E1 = 8, 4
    RANK = 16
    SCALE0, SCALE1 = 32.0 / RANK, 16.0 / math.sqrt(16.0)
    HEADS, WINDOW = 8, 16
    HD = P // HEADS
    QB = 16
    NBLK = D // QB
    KEYS = 2 * QB
    PAD = WINDOW // 2
    NG = 4
    GB = NBLK // NG
    GW = GB * QB
    ATT_SCALE = HD ** -0.5
    TOPK = int(2 * np.log(P))
    assert TOPK == 9 and D == 1024

    ctx = ExitStack()
    with ctx:
        def sb(name, shape, dt=F32):
            return ctx.enter_context(nc.sbuf_tensor(name, shape, dt))

        small = sb("small", [P, 256])
        small_used = []

        def little(*shape):
            at, size = sum(small_used), math.prod(shape)
            small_used.append(size)
            assert at + size <= 256
            columns = small[:, at:at + size]
            return columns if len(shape) == 1 else columns.rearrange("p (a b) -> p a b", b=shape[1])

        def signal(name, per=1):
            return Signal(ctx.enter_context(nc.semaphore(name)), per)

        tab = sb("tab", [P, 9, P])
        ident = sb("ident", [P, P])
        ident_bf = sb("ident_bf", [P, P], BF16)
        band_mask = sb("band_mask", [P, KEYS])
        band_bf = sb("band_bf", [P, KEYS], BF16)
        par = sb("par", [P, 2])
        w_base_h = sb("w_base_h", [P, KT, D], F16)
        w_base_l = sb("w_base_l", [P, KT, D], F16)
        bias_base = sb("bias_base", [P, D])
        w_ra0_h = sb("w_ra0_h", [P, KT, E0 + P], F16)
        w_ra0_l = sb("w_ra0_l", [P, KT, E0 + P], F16)
        w_b0 = sb("w_b0", [P, D])
        w_att = sb("w_att", [P, 4, P])
        bias_att = sb("bias_att", [P, 4])
        w_ra1 = sb("w_ra1", [P, KT, E1 + E1 * RANK])
        w_b1 = sb("w_b1", [E1 * RANK, D])

        x_a = sb("x_a", [P, D])
        x_res = sb("x_res", [P, D])
        ctx_a = sb("ctx_a", [P, D])
        xn_a = sb("xn_a", [P, D])
        wt = xn_a
        q_spec = sb("q_spec", [P, D])
        v_re = sb("v_re", [P, D])
        v_im = sb("v_im", [P, D])
        rest = sb("rest", [P, KT, P])
        rest_flat = rest[:, :, :].rearrange("p a b -> p (a b)")
        prob = sb("prob", [P, KT, P])
        prob_flat = prob[:, :, :].rearrange("p a b -> p (a b)")
        c1, c2 = xn_a, rest_flat
        agg_re, agg_im = rest_flat, prob_flat
        top8 = sb("top8", [P, KT, 8])
        ninth = sb("ninth", [P, KT, 8])
        neg_max = sb("neg_max", [P, KT])
        psum_w = sb("psum_w", [P, KT])
        rec_w = sb("rec_w", [P, KT])

        x_b = sb("x_b", [P, D])
        ctx_b = sb("ctx_b", [P, D])
        xn_b = sb("xn_b", [P, D])
        even_words = sb("even_words", [P, D])
        xt_h = even_words[:, :].bitcast(F16)[:, 0:D]
        xt_l = even_words[:, :].bitcast(F16)[:, D:2 * D]
        k_h = sb("k_h", [P, D + 2 * PAD], F16)
        k_l = sb("k_l", [P, D + 2 * PAD], F16)
        v_pad = sb("v_pad", [P, D + 2 * PAD])
        q_diag = sb("q_diag", [P, NBLK, P])
        v_diag = sb("v_diag", [P, NBLK, 2, P // 2])

        x_c = sb("x_c", [P, D])
        sc = sb("sc", [P, 2, GB, KEYS])
        p_hl = sb("p_hl", [P, 2, GB, KEYS])
        sc_t = sb("sc_t", [P, 2, GB, KEYS])
        rows_c = sb("rows_c", [P, D])
        sc_max = sb("sc_max", [P, NBLK])
        sc_sum = sb("sc_sum", [P, NBLK])
        sc_rec = sb("sc_rec", [P, NBLK])

        q_hl = sc[:, :, :, :].rearrange("p a n k -> p (a n k)")
        v_t = [even_words[:, :], p_hl[:, :, :, :].rearrange("p a n k -> p (a n k)")]
        xt_c = sc_t[:, :, :, :].rearrange("p a n k -> p (a n k)")
        xn_c = v_t[1]

        lg = [little(16) for n in range(2)]
        lg_top = [little(8) for n in range(2)]
        lg_pick = [little(8) for n in range(2)]
        lg_mark = [little(16) for n in range(2)]
        lg_neg = [little(1) for n in range(2)]
        lg_exp = [little(E0) for n in range(2)]
        gate = [little(E0) for n in range(2)]
        gate_sum = [little(1) for n in range(2)]
        gate_rec = [little(1) for n in range(2)]
        mid = [sb(f"mid{n}", [P, [P, E1 * RANK][n]]) for n in range(2)]
        mid_t = [sb(f"mid_t{n}", [[P, E1 * RANK][n], P]) for n in range(2)]

        bn = [little(2, 6) for n in range(4)]
        mv = [little(2) for n in range(4)]
        rs_v = [little(1) for n in range(4)]
        rs_t = [little(1) for n in range(4)]
        rs_u = [little(1) for n in range(4)]
        rs_y = [little(1) for n in range(4)]
        idle_dve = little(9)
        one = little(1)

        def psum(name, banks):
            return ctx.enter_context(nc.psum_tensor(name, [P, banks, HALF], F32))

        def flat(t):
            return t.rearrange("p a b -> p (a b)")

        pa = psum("pa", 4)
        pb = psum("pb", 2)
        pc = psum("pc", 2)
        pa_lo, pa_hi = flat(pa[:, 0:2, :]), flat(pa[:, 2:4, :])
        pb_all, pc_all = flat(pb[:, :, :]), flat(pc[:, :, :])
        MID_AT = 256

        tab_in = signal("tab_in")
        const_in = signal("const_in")
        w_in = signal("w_in")
        const_set = signal("const_set")
        diag_set = signal("diag_set")
        w_hi = signal("w_hi")
        w_lo = signal("w_lo")
        x_in = signal("x_in", 16)
        xres_in = signal("xres_in", 16)
        ctxa_in = signal("ctxa_in", 16)
        ctxb_in = signal("ctxb_in", 16)
        out_done = signal("out_done", 16)
        ln_bn = [signal(f"ln_bn{n}", 2) for n in range(4)]
        ln_mv = [signal(f"ln_mv{n}") for n in range(4)]
        ln_rs = [signal(f"ln_rs{n}", RSQRT_STEPS) for n in range(4)]
        ln_out = [signal(f"ln_out{n}") for n in range(4)]
        mm_ctx = signal("mm_ctx")
        mm_q = signal("mm_q")
        v_out = signal("v_out", 4)
        mm_vagg = signal("mm_vagg", 2)
        vagg_out = signal("vagg_out", 2)
        q_out = signal("q_out")
        prod_q = signal("prod_q")
        prod_q2 = signal("prod_q2")
        mm_corr = signal("mm_corr", 2)
        top_found = signal("top_found", KT)
        top_gone = signal("top_gone", KT)
        negmax_out = signal("negmax_out", 2)
        ninth_found = signal("ninth_found")
        ninth_gone = signal("ninth_gone", KT)
        exp_out = signal("exp_out", KT)
        prob_masked = signal("prob_masked", KT)
        rec_out = signal("rec_out")
        prob_out = signal("prob_out")
        tr_w = signal("tr_w", 2)
        wt_out = signal("wt_out", 2)
        mm_wre = signal("mm_wre")
        mm_wim = signal("mm_wim")
        prod_w = signal("prod_w", 4)
        sum_w = signal("sum_w", 2)
        mm_agg = signal("mm_agg")
        x1_out = signal("x1_out")
        tr_x = [signal(f"tr_x{n}", 2) for n in range(2)]
        xt_out = [signal(f"xt_out{n}", 2) for n in range(2)]
        xtl_out = signal("xtl_out", 2)
        mm_ra = [signal(f"mm_ra{n}") for n in range(2)]
        gt = [signal(f"gt{n}", 8) for n in range(2)]
        gt_exp = [signal(f"gt_exp{n}") for n in range(2)]
        mid_out = [signal(f"mid_out{n}") for n in range(2)]
        tr_mid = [signal(f"tr_mid{n}") for n in range(2)]
        midt_out = [signal(f"midt_out{n}") for n in range(2)]
        mm_ffn = [signal(f"mm_ffn{n}") for n in range(2)]
        bias_added = signal("bias_added")
        x2_out = signal("x2_out")
        x2_moved = signal("x2_moved")
        x4_out = signal("x4_out")
        mm_k = signal("mm_k")
        mm_v = signal("mm_v")
        mm_qq = signal("mm_qq")
        kh_out = signal("kh_out")
        kl_out = signal("kl_out")
        vh_out = signal("vh_out")
        vl_out = signal("vl_out")
        qh_out = signal("qh_out")
        ql_out = signal("ql_out")
        vt_out = signal("vt_out", 2)
        PAIRS = HEADS // 2
        POOL_PAIR = PAIRS - 1
        vd_out = signal("vd_out", 2 * (PAIRS - 1))
        vd_pool = signal("vd_pool", 2)
        qd_out = signal("qd_out", 2 * (PAIRS - 1))
        qd_pool = signal("qd_pool", 2)
        mm_sc = signal("mm_sc", NG)
        max_out = signal("max_out", NG)
        sc_in = signal("sc_in", NG)
        sc_exp = signal("sc_exp", NG)
        sum_out = signal("sum_out", NG)
        srec_out = signal("srec_out", NG)
        p_out = signal("p_out", NG)
        ph_out = signal("ph_out", NG)
        pl_out = signal("pl_out", NG)
        pt_out = signal("pt_out", NG)
        mm_av = signal("mm_av", NG)
        av_out = signal("av_out", 2 * NG)
        mm_o = signal("mm_o")
        x3_out = signal("x3_out")

        tables = [(tab, spectra), (ident, identity), (band_mask, band), (par, parity)]
        consts = [(w_b0, b0), (w_att, wqkvo), (bias_att, biases), (w_ra1, ra1), (w_b1, b1)]
        TABLES_IN = 16 * len(tables)
        CONSTS_IN = 16 * (len(consts) + 1)
        CONSTS_SET = 10
        WEIGHTS_SPLIT = 2

        base_f32 = v_diag[:, :, :, :].rearrange("p n a c -> p (n a c)")
        ra0_f32 = q_diag[:, :, :].rearrange("p n c -> p (n c)")[:, 0:KT * (E0 + P)]

        idle_column = {}

        def dve_wait(dve, signal, value):
            column = idle_column.setdefault(signal, len(idle_column))
            dve.wait_ge(signal.sem, value)
            nc.vector.memset(idle_dve[:, column:column + 1], 0.0)

        block = ctx.enter_context(nc.Block())

        @block.sync
        def _(sp):
            def load_x(b):
                if not first(b):
                    sp.wait_ge(ln_out[0].sem, ln_out[0].after(b - 1))
                sp.dma_start(x_a[:, :], x[b]).then_inc(x_in.sem, 16)

            def load_x_res(b):
                if not first(b):
                    sp.wait_ge(x1_out.sem, x1_out.after(b - 1))
                sp.dma_start(x_res[:, :], x[b]).then_inc(xres_in.sem, 16)

            def load_ctx_a(b):
                if not first(b):
                    sp.wait_ge(mm_vagg.sem, mm_vagg.after(b - 1))
                sp.dma_start(ctx_a[:, :], ctx_in[b]).then_inc(ctxa_in.sem, 16)

            def load_ctx_b(b):
                if not first(b):
                    sp.wait_ge(mm_v.sem, mm_v.after(b - 1))
                sp.dma_start(ctx_b[:, :], ctx_in[b]).then_inc(ctxb_in.sem, 16)

            def store(b):
                sp.wait_ge(x4_out.sem, x4_out.after(b))
                sp.dma_start(out[b], rows_c[:, :]).then_inc(out_done.sem, 16)

            load_x(0)
            load_ctx_a(0)
            sp.dma_start(tab[:], spectra).then_inc(tab_in.sem, 16)
            for place, source in tables[1:]:
                sp.dma_start(place[:], source).then_inc(tab_in.sem, 16)
            load_x(1)
            load_x_res(0)
            sp.dma_start(base_f32, base_w.rearrange("p k n -> p (k n)")).then_inc(w_in.sem, 16)
            sp.dma_start(ra0_f32, ra0.rearrange("p k n -> p (k n)")).then_inc(w_in.sem, 16)
            for place, source in consts:
                sp.dma_start(place[:], source).then_inc(const_in.sem, 16)
            sp.dma_start(bias_base[:, :], base_b.partition_broadcast(P)).then_inc(const_in.sem, 16)
            load_ctx_b(0)

            def step(i, do_a, do_x, do_c):
                if do_a:
                    load_ctx_a(i + 1)
                if do_x:
                    load_x(i + 2)
                if not first(i):
                    load_ctx_b(i)
                if do_c:
                    store(i - 2)
                if do_a:
                    load_x_res(i + 1)

            step(0, True, True, False)
            step(1, True, True, False)
            with sp.Fori(2, BATCH - 2) as i:
                step(i, True, True, True)
            step(BATCH - 2, True, False, True)
            step(BATCH - 1, False, False, True)
            store(BATCH - 2)
            store(BATCH - 1)
            sp.wait_ge(out_done.sem, out_done.after(BATCH - 1))

        @block.tensor
        def _(pe):
            mm = nc.tensor.matmul

            def project(place, n, moving, lhsT):
                for h in range(2):
                    last = mm(place[:, n + h, :], lhsT, moving[:, h * HALF:(h + 1) * HALF],
                              start=True, stop=True)
                return last

            def a_context(b):
                pe.wait_ge(ctxa_in.sem, ctxa_in.after(b))
                if not first(b):
                    pe.wait_ge(x1_out.sem, x1_out.after(b - 1))
                project(pa, 0, ctx_a, tab[:, FWD, :]).then_inc(mm_ctx.sem, 1)

            def a_query(b):
                if not first(b):
                    pe.wait_ge(prod_w.sem, prod_w.after(b - 1))
                pe.wait_ge(ln_out[0].sem, ln_out[0].after(b))
                project(pa, 2, xn_a, tab[:, FWD, :]).then_inc(mm_q.sem, 1)

            def a_corr(b, h):
                if h == 0:
                    pe.wait_ge(prod_q.sem, prod_q.after(b))
                    pe.wait_ge(prod_q2.sem, prod_q2.after(b))
                    pe.wait_ge(v_out.sem, v_out.after(b))
                for j in range(4 * h, 4 * h + 4):
                    place = pa[:, h, (j % 4) * P:(j % 4 + 1) * P]
                    mm(place, c1[:, j * P:(j + 1) * P], tab[:, CORR_1, :], start=True, stop=False)
                    last = mm(place, c2[:, j * P:(j + 1) * P], tab[:, CORR_2, :], start=False, stop=True)
                last.then_inc(mm_corr.sem, 1)

            def a_context_long(b, n):
                if n == 0:
                    pe.wait_ge(q_out.sem, q_out.after(b))
                else:
                    pe.wait_ge(vagg_out.sem, vagg_out.after(b, n))
                project(pa, 2, ctx_a, tab[:, [CTX_RE, CTX_IM][n], :]).then_inc(mm_vagg.sem, 1)

            def a_transpose(b):
                pe.wait_ge(prob_out.sem, prob_out.after(b))
                pe.wait_ge(vagg_out.sem, vagg_out.after(b))
                for j in range(KT):
                    place = pa[:, 2 + j // 4, (j % 4) * P:(j % 4 + 1) * P]
                    last = nc.tensor.transpose(place, prob[:, j, :], ident[:, :])
                    if j % 4 == 3:
                        last.then_inc(tr_w.sem, 1)

            def a_weights(b, n):
                if n == 0:
                    pe.wait_ge(wt_out.sem, wt_out.after(b))
                    project(pa, 2, wt, tab[:, WEIGHTS_IM, :]).then_inc(mm_wim.sem, 1)
                else:
                    pe.wait_ge(wt_out.sem, wt_out.after(b))
                    pe.wait_ge(exp_out.sem, exp_out.after(b))
                    project(pa, 0, wt, tab[:, WEIGHTS_RE, :]).then_inc(mm_wre.sem, 1)

            def a_aggregate(b, n):
                pe.wait_ge(sum_w.sem, sum_w.after(b, n + 1))
                for h in range(2):
                    last = mm(pa[:, h, :], tab[:, [AGG_RE, AGG_IM][n], :],
                              [agg_re, agg_im][n][:, h * HALF:(h + 1) * HALF], start=(n == 0), stop=(n == 1))
                if n == 1:
                    last.then_inc(mm_agg.sem, 1)

            def rows_to_features(b, n, ln, source, place):
                pe.wait_ge(ln_out[ln].sem, ln_out[ln].after(b))
                if n == 0:
                    if not first(b):
                        pe.wait_ge(ql_out.sem, ql_out.after(b - 1))
                else:
                    pe.wait_ge(x3_out.sem, x3_out.after(b))
                for j in range(KT):
                    last = nc.tensor.transpose(place[:, j // 4, (j % 4) * P:(j % 4 + 1) * P],
                                               source[:, j * P:(j + 1) * P], ident[:, :])
                    if j % 4 == 3:
                        last.then_inc(tr_x[n].sem, 1)

            def b_router(b):
                if first(b):
                    pe.wait_ge(w_lo.sem, WEIGHTS_SPLIT)
                pe.wait_ge(xtl_out.sem, xtl_out.after(b))
                n = 0
                for j in range(KT):
                    cols = slice(j * P, (j + 1) * P)
                    for rows, weights in ((xt_h, w_ra0_h), (xt_h, w_ra0_l), (xt_l, w_ra0_h)):
                        n += 1
                        last = mm(pb[:, 0, 0:E0 + P], rows[:, cols], weights[:, j, :],
                                  start=(n == 1), stop=(n == 3 * KT))
                last.then_inc(mm_ra[0].sem, 1)

            def b_base(b, h, part):
                if h == 0 and part == 0:
                    pe.wait_ge(midt_out[0].sem, midt_out[0].after(b))
                for j in range(part * KT // 2, (part + 1) * KT // 2):
                    cols = slice(j * P, (j + 1) * P)
                    for m, (rows, weights) in enumerate(((xt_h, w_base_h), (xt_h, w_base_l), (xt_l, w_base_h))):
                        mm(pb[:, h, :], rows[:, cols], weights[:, j, h * HALF:(h + 1) * HALF],
                           start=(j == 0 and m == 0), stop=False)

            def b_base_end(b):
                for h in range(2):
                    last = mm(pb[:, h, :], mid_t[0][:, :], w_b0[:, h * HALF:(h + 1) * HALF],
                              start=False, stop=True)
                last.then_inc(mm_ffn[0].sem, 1)

            def b_mid(b):
                pe.wait_ge(mid_out[0].sem, mid_out[0].after(b))
                nc.tensor.transpose(pb[:, 0, MID_AT:MID_AT + P], mid[0][:, :], ident[:, :])\
                    .then_inc(tr_mid[0].sem, 1)

            def b_keys(b):
                pe.wait_ge(ctxb_in.sem, ctxb_in.after(b))
                pe.wait_ge(x2_out.sem, x2_out.after(b))
                project(pb, 0, ctx_b, w_att[:, 1, :]).then_inc(mm_k.sem, 1)

            def b_values(b):
                pe.wait_ge(kl_out.sem, kl_out.after(b))
                project(pb, 0, ctx_b, w_att[:, 2, :]).then_inc(mm_v.sem, 1)

            def b_queries(b):
                pe.wait_ge(ln_out[2].sem, ln_out[2].after(b))
                pe.wait_ge(vl_out.sem, vl_out.after(b))
                project(pb, 0, xn_b, w_att[:, 0, :]).then_inc(mm_qq.sem, 1)

            q_halves = words(q_diag[:, :, :])

            def c_scores(b, g):
                if g == 0:
                    pe.wait_ge(qd_out.sem, qd_out.after(b))
                    pe.wait_ge(qd_pool.sem, qd_pool.after(b))
                    if not first(b):
                        pe.wait_ge(x4_out.sem, x4_out.after(b - 1))
                else:
                    pe.wait_ge(sc_in.sem, sc_in.after(b, g))
                mm(pc[:, 0, :], ident_bf[:, :], band_bf[:, :].unsqueeze(1).to_broadcast([P, GB, KEYS]),
                   start=True, stop=False)
                for i in range(GB):
                    blk = g * GB + i
                    place = pc[:, 0, i * KEYS:(i + 1) * KEYS]
                    keys = slice(blk * QB, blk * QB + KEYS)
                    mm(place, q_halves[:, blk, :, HI], k_h[:, keys], start=False, stop=False)
                    mm(place, q_halves[:, blk, :, HI], k_l[:, keys], start=False, stop=False)
                    last = mm(place, q_halves[:, blk, :, LO], k_h[:, keys], start=False, stop=(i == GB - 1))
                last.then_inc(mm_sc.sem, 1)

            p_halves = words(sc_t[:, :, :, :])
            v_halves = words(v_diag[:, :, :, :].rearrange("p n a c -> p n (a c)"))

            def c_attend(b, g):
                pe.wait_ge(pt_out.sem, pt_out.after(b, g + 1))
                if g == 0:
                    pe.wait_ge(vd_out.sem, vd_out.after(b))
                    pe.wait_ge(vd_pool.sem, vd_pool.after(b))
                    if not first(b):
                        pe.wait_ge(x4_out.sem, x4_out.after(b - 1))
                else:
                    pe.wait_ge(av_out.sem, av_out.after(b, 2 * g))
                for i in range(GB):
                    blk = g * GB + i
                    place = pc[:, 1, i * KEYS:(i + 1) * KEYS]
                    for m, (v_part, p_part) in enumerate(((HI, HI), (HI, LO), (LO, HI))):
                        last = mm(place, v_halves[:, blk, :, v_part], p_halves[:, g % 2, i, :, p_part],
                                  start=(m == 0), stop=(m == 2))
                last.then_inc(mm_av.sem, 1)

            def c_output(b):
                pe.wait_ge(av_out.sem, av_out.after(b))
                pe.wait_ge(sc_in.sem, sc_in.after(b))
                project(pc, 0, rows_c, w_att[:, 3, :]).then_inc(mm_o.sem, 1)

            def c_router(b):
                pe.wait_ge(xt_out[1].sem, xt_out[1].after(b))
                for j in range(KT):
                    last = mm(pc[:, 0, 0:E1 + E1 * RANK], xt_c[:, j * P:(j + 1) * P], w_ra1[:, j, :],
                              start=(j == 0), stop=(j == KT - 1))
                last.then_inc(mm_ra[1].sem, 1)

            def c_mid(b):
                pe.wait_ge(mid_out[1].sem, mid_out[1].after(b))
                nc.tensor.transpose(pc[:, 0, 384:384 + P], ident[:, :], ident[:, :])
                nc.tensor.transpose(pc[0:E1 * RANK, 0, MID_AT:MID_AT + P], mid[1][:, :], ident[:, :])\
                    .then_inc(tr_mid[1].sem, 1)

            def c_delta(b):
                pe.wait_ge(midt_out[1].sem, midt_out[1].after(b))
                for h in range(2):
                    last = mm(pc[:, h, :], mid_t[1][:, :], w_b1[:, h * HALF:(h + 1) * HALF],
                              start=True, stop=True)
                last.then_inc(mm_ffn[1].sem, 1)

            def step(i, do_a, do_b, do_c):
                b, c = i - 1, i - 2
                if do_a:
                    a_context(i)
                if do_c:
                    c_scores(c, 0)
                if do_a:
                    a_query(i)
                if do_c:
                    c_scores(c, 1)
                if do_b:
                    rows_to_features(b, 0, 1, xn_b, pb)
                if do_c:
                    c_scores(c, 2)
                if do_a:
                    a_context_long(i, 0)
                if do_b:
                    b_router(b)
                    b_base(b, 1, 0)
                if do_c:
                    c_scores(c, 3)
                if do_b:
                    b_mid(b)
                if do_c:
                    c_attend(c, 0)
                if do_b:
                    b_base(b, 0, 0)
                if do_a:
                    a_corr(i, 0)
                    a_corr(i, 1)
                if do_c:
                    c_attend(c, 1)
                if do_b:
                    b_base(b, 0, 1)
                if do_c:
                    c_attend(c, 2)
                if do_b:
                    b_base(b, 1, 1)
                    b_base_end(b)
                if do_c:
                    c_attend(c, 3)
                if do_a:
                    a_context_long(i, 1)
                if do_c:
                    c_output(c)
                if do_b:
                    b_keys(b)
                if do_a:
                    a_transpose(i)
                    a_weights(i, 1)
                if do_b:
                    b_values(b)
                if do_a:
                    a_weights(i, 0)
                if do_c:
                    rows_to_features(c, 1, 3, xn_c, pc)
                if do_b:
                    b_queries(b)
                if do_c:
                    c_router(c)
                if do_a:
                    a_aggregate(i, 0)
                    a_aggregate(i, 1)
                if do_c:
                    c_mid(c)
                    c_delta(c)

            pe.wait_ge(tab_in.sem, TABLES_IN)
            step(0, True, False, False)
            pe.wait_ge(const_in.sem, CONSTS_IN)
            pe.wait_ge(const_set.sem, CONSTS_SET)
            step(1, True, True, False)
            step(2, True, True, True)
            with pe.Fori(3, BATCH) as i:
                step(i, True, True, True)
            step(BATCH, False, True, True)
            step(BATCH + 1, False, False, True)

        @block.scalar
        def _(act):
            def copy(dst, src):
                return nc.scalar.activation(dst, src, ACT.Copy)

            def twice(place, part, signal):
                rows = slice(part * P // 2, (part + 1) * P // 2)
                for half in range(2):
                    copy(place[half * P // 2:(half + 1) * P // 2, :], pa_lo[rows, :]).then_inc(signal.sem, 1)

            def a_values(b, n):
                if n == 0:
                    act.wait_ge(mm_ctx.sem, mm_ctx.after(b))
                    if not first(b):
                        act.wait_ge(mm_agg.sem, mm_agg.after(b - 1))
                twice([v_re, v_im][n], n, v_out)

            def a_values_long(b, n):
                act.wait_ge(mm_vagg.sem, mm_vagg.after(b, n + 1))
                if n == 0:
                    act.wait_ge(prod_q.sem, prod_q.after(b))
                else:
                    act.wait_ge(prod_q2.sem, prod_q2.after(b))
                copy([v_re, v_im][n][:, :], pa_hi).then_inc(vagg_out.sem, 1)

            def a_query(b):
                act.wait_ge(mm_q.sem, mm_q.after(b))
                copy(q_spec[:, :], pa_hi).then_inc(q_out.sem, 1)

            def a_exp(b, h):
                act.wait_ge(negmax_out.sem, negmax_out.after(b, h + 1))
                for j in range(4 * h, 4 * h + 4):
                    nc.scalar.activation(prob[:, j, :], pa[:, h, (j % 4) * P:(j % 4 + 1) * P], ACT.Exp,
                                         bias=neg_max[:, j:j + 1]).then_inc(exp_out.sem, 1)

            def a_transposed(b, h):
                act.wait_ge(tr_w.sem, tr_w.after(b, h + 1))
                copy(wt[:, h * HALF:(h + 1) * HALF], pa[:, 2 + h, :]).then_inc(wt_out.sem, 1)

            def b_features(b, h):
                if h == 0 and not first(b):
                    act.wait_ge(vd_out.sem, vd_out.after(b - 1))
                    act.wait_ge(vd_pool.sem, vd_pool.after(b - 1))
                act.wait_ge(tr_x[0].sem, tr_x[0].after(b, h + 1))
                copy(xt_h[:, h * HALF:(h + 1) * HALF], pb[:, h, :]).then_inc(xt_out[0].sem, 1)

            def b_keys(b):
                act.wait_ge(mm_k.sem, mm_k.after(b))
                if not first(b):
                    act.wait_ge(mm_sc.sem, mm_sc.after(b - 1))
                nc.scalar.activation(k_h[:, PAD:PAD + D], pb_all, ACT.Identity, bias=bias_att[:, 1:2])\
                    .then_inc(kh_out.sem, 1)

            v_halves = words(v_pad[:, :])

            def b_values(b):
                act.wait_ge(mm_v.sem, mm_v.after(b))
                nc.scalar.activation(v_halves[:, PAD:PAD + D, HI], pb_all, ACT.Identity,
                                     bias=bias_att[:, 2:3]).then_inc(vh_out.sem, 1)

            def b_value_blocks(b, odd, pair):
                if pair == 0:
                    act.wait_ge(vt_out.sem, vt_out.after(b, odd + 1))
                    if odd == 0:
                        act.wait_ge(diag_set.sem, 2)
                        if not first(b):
                            act.wait_ge(mm_av.sem, mm_av.after(b - 1))
                rows = slice(32 * pair, 32 * pair + 32)
                place = v_diag[rows, :, :, pair * HD:(pair + 1) * HD]\
                    .rearrange("p (m o) a d -> p o m a d", o=2)[:, odd]
                copy(place, v_t[odd][rows, :].rearrange("p (m a d) -> p m a d", a=2, d=HD))\
                    .then_inc(vd_out.sem, 1)

            def b_queries(b):
                act.wait_ge(mm_qq.sem, mm_qq.after(b))
                if not first(b):
                    act.wait_ge(pl_out.sem, pl_out.after(b - 1))
                nc.scalar.activation(words(q_hl)[:, :, HI], pb_all, ACT.Identity, bias=bias_att[:, 0:1])\
                    .then_inc(qh_out.sem, 1)

            def b_query_blocks(b, pair, a):
                if pair == 0 and a == 0:
                    act.wait_ge(ql_out.sem, ql_out.after(b))
                    act.wait_ge(diag_set.sem, 2)
                    if not first(b):
                        act.wait_ge(mm_sc.sem, mm_sc.after(b - 1))
                rows = slice(32 * pair, 32 * pair + 32)
                source = q_hl[rows, :].rearrange("p (n t) -> p n t", t=QB)
                col = (2 * pair + a) * QB
                nc.scalar.activation(q_diag[rows, :, col:col + QB], source, ACT.Copy,
                                     scale=par[rows, a:a + 1]).then_inc(qd_out.sem, 1)

            def experts_exp(b, n, experts):
                act.wait_ge(gt[n].sem, gt[n].after(b, 5))
                nc.scalar.activation(lg_exp[n][:, 0:experts], lg[n][:, 0:experts], ACT.Exp,
                                     bias=lg_neg[n][:, :]).then_inc(gt_exp[n].sem, 1)

            def experts_mid(b, n, source, rows):
                act.wait_ge(tr_mid[n].sem, tr_mid[n].after(b))
                copy(mid_t[n][:, :], source[0:rows, 0, MID_AT:MID_AT + P]).then_inc(midt_out[n].sem, 1)

            def c_exp(b, g):
                act.wait_ge(sc_in.sem, sc_in.after(b, g + 1))
                nc.scalar.activation(sc[:, g % 2, :, :], sc[:, g % 2, :, :], ACT.Exp, scale=ATT_SCALE)\
                    .then_inc(sc_exp.sem, 1)

            def c_high(b, g):
                act.wait_ge(p_out.sem, p_out.after(b, g + 1))
                copy(words(p_hl[:, g % 2, :, :])[:, :, :, HI], sc[:, g % 2, :, :]).then_inc(ph_out.sem, 1)

            def c_attended(b, g):
                act.wait_ge(mm_av.sem, mm_av.after(b, g + 1))
                if g == 0 and not first(b):
                    act.wait_ge(out_done.sem, out_done.after(b - 1))
                for a in range(2):
                    rows = slice(64 * a, 64 * a + 64)
                    copy(rows_c[rows, g * GW:(g + 1) * GW].rearrange("p (n t) -> p n t", t=QB),
                         pc[rows, 1, :].rearrange("p (n s) -> p n s", s=KEYS)[:, :, a * QB:(a + 1) * QB])\
                        .then_inc(av_out.sem, 1)

            def c_features(b, h):
                act.wait_ge(tr_x[1].sem, tr_x[1].after(b, h + 1))
                copy(xt_c[:, h * HALF:(h + 1) * HALF], pc[:, h, :]).then_inc(xt_out[1].sem, 1)

            def step(i, do_a, do_b, do_c):
                b, c = i - 1, i - 2
                if do_c:
                    c_exp(c, 0)
                if do_a:
                    a_values(i, 0)
                    a_query(i)
                if do_b:
                    b_features(b, 0)
                    b_features(b, 1)
                if do_c:
                    c_exp(c, 1)
                    c_high(c, 0)
                if do_a:
                    a_values(i, 1)
                if do_c:
                    c_exp(c, 2)
                if do_b:
                    experts_exp(b, 0, E0)
                    experts_mid(b, 0, pb, P)
                if do_c:
                    c_high(c, 1)
                if do_a:
                    a_values_long(i, 0)
                if do_c:
                    c_attended(c, 0)
                    c_high(c, 2)
                    c_exp(c, 3)
                    c_high(c, 3)
                if do_a:
                    a_exp(i, 0)
                if do_c:
                    c_attended(c, 1)
                    c_attended(c, 2)
                if do_a:
                    a_exp(i, 1)
                if do_c:
                    c_attended(c, 3)
                if do_a:
                    a_values_long(i, 1)
                if do_b:
                    b_keys(b)
                if do_a:
                    a_transposed(i, 0)
                    a_transposed(i, 1)
                if do_b:
                    b_values(b)
                if do_c:
                    c_features(c, 0)
                    c_features(c, 1)
                if do_b:
                    b_queries(b)
                    b_value_blocks(b, 0, 0)
                    b_query_blocks(b, 0, 0)
                if do_c:
                    experts_exp(c, 1, E1)
                if do_b:
                    b_query_blocks(b, 0, 1)
                    b_query_blocks(b, 1, 0)
                if do_c:
                    experts_mid(c, 1, pc, E1 * RANK)
                if do_b:
                    b_query_blocks(b, 1, 1)
                    b_query_blocks(b, 2, 0)
                    b_query_blocks(b, 2, 1)
                    b_value_blocks(b, 0, 1)
                    b_value_blocks(b, 0, 2)
                    b_value_blocks(b, 1, 0)
                    b_value_blocks(b, 1, 1)
                    b_value_blocks(b, 1, 2)

            act.wait_ge(tab_in.sem, TABLES_IN)
            act.wait_ge(const_set.sem, CONSTS_SET)
            step(0, True, False, False)
            act.wait_ge(w_in.sem, 32)
            for part, whole in ((w_base_h, base_f32), (w_ra0_h, ra0_f32)):
                nc.scalar.activation(part[:, :, :].rearrange("p k n -> p (k n)"), whole, ACT.Copy,
                                     scale=W_SCALE).then_inc(w_hi.sem, 1)
            act.wait_ge(const_in.sem, CONSTS_IN)
            step(1, True, True, False)
            step(2, True, True, True)
            with act.Fori(3, BATCH) as i:
                step(i, True, True, True)
            step(BATCH, False, True, True)
            step(BATCH + 1, False, False, True)

        @block.vector
        def _(dve):
            v = nc.vector

            def layer_norm(b, n, rows):
                for h in range(2):
                    v.bn_stats(bn[n][:, h, :], rows[:, h * HALF:(h + 1) * HALF]).then_inc(ln_bn[n].sem, 1)

            def variance(b, n):
                dve_wait(dve, ln_bn[n], ln_bn[n].after(b))
                v.bn_aggr(mv[n][:, :], bn[n][:, :, :]).then_inc(ln_mv[n].sem, 1)

            def root(b, n, k):
                var, t, u, y = rs_v[n][:, :], rs_t[n][:, :], rs_u[n][:, :], rs_y[n][:, :]
                steps = ln_rs[n]
                if k == 0:
                    dve.wait_ge(ln_mv[n].sem, ln_mv[n].after(b))
                    v.tensor_scalar(var, mv[n][:, 1:2], 1e-5, 4.0 * RSQRT_K ** 6, ALU.add, ALU.mult)\
                        .then_inc(steps.sem, 1)
                    return
                dve.wait_ge(steps.sem, steps.after(b, k))
                if k == 1:
                    v.tensor_scalar(y.bitcast(I32), var.bitcast(I32), -0.5, float(RSQRT_MAGIC),
                                    ALU.mult, ALU.add).then_inc(steps.sem, 1)
                elif k in (2, 5):
                    v.scalar_tensor_tensor(out=t, in0=y, scalar=y, in1=var, op0=ALU.mult, op1=ALU.mult)\
                        .then_inc(steps.sem, 1)
                elif k == 3:
                    v.scalar_tensor_tensor(out=u, in0=t, scalar=-10.0 / 3.0, in1=t, op0=ALU.add, op1=ALU.mult)\
                        .then_inc(steps.sem, 1)
                elif k == 4:
                    v.scalar_tensor_tensor(out=y, in0=u, scalar=5.0, in1=y, op0=ALU.add, op1=ALU.mult)\
                        .then_inc(steps.sem, 1)
                else:
                    v.scalar_tensor_tensor(out=y, in0=t, scalar=-3.0 * RSQRT_K ** 2, in1=y,
                                           op0=ALU.add, op1=ALU.mult).then_inc(steps.sem, 1)

            def normalise(b, n, rows, place):
                dve.wait_ge(ln_rs[n].sem, ln_rs[n].after(b))
                v.tensor_scalar(place[:, :], rows[:, :], mv[n][:, 0:1], rs_y[n][:, :],
                                ALU.subtract, ALU.mult).then_inc(ln_out[n].sem, 1)

            def a_norm(b):
                dve.wait_ge(x_in.sem, x_in.after(b))
                layer_norm(b, 0, x_a)

            def a_norm_rows(b):
                if not first(b):
                    dve.wait_ge(mm_wre.sem, mm_wre.after(b - 1))
                    dve.wait_ge(mm_wim.sem, mm_wim.after(b - 1))
                normalise(b, 0, x_a, xn_a)

            def a_product(b):
                dve.wait_ge(q_out.sem, q_out.after(b))
                dve.wait_ge(v_out.sem, v_out.after(b, 2))
                v.tensor_tensor(c1[:, :], q_spec[:, :], v_re[:, :], ALU.mult).then_inc(prod_q.sem, 1)

            def a_top(b, h):
                dve_wait(dve, mm_corr, mm_corr.after(b, h + 1))
                for j in range(4 * h, 4 * h + 4):
                    v.max(top8[:, j, :], pa[:, h, (j % 4) * P:(j % 4 + 1) * P]).then_inc(top_found.sem, 1)
                dve_wait(dve, top_found, top_found.after(b, 4 * h + 4))
                for j in range(4 * h, 4 * h + 4):
                    v.match_replace(rest[:, j, :], top8[:, j, :], pa[:, h, (j % 4) * P:(j % 4 + 1) * P],
                                    GONE).then_inc(top_gone.sem, 1)
                dve.wait_ge(top_gone.sem, top_gone.after(b, 4 * h + 4))
                v.tensor_scalar(neg_max[:, 4 * h:4 * h + 4], top8[:, 4 * h:4 * h + 4, 0], -1.0, None,
                                ALU.mult).then_inc(negmax_out.sem, 1)

            def a_ninth(b):
                v.tensor_reduce(ninth[:, :, 0], rest[:, :, :], AX_X, ALU.max).then_inc(ninth_found.sem, 1)
                dve_wait(dve, ninth_found, ninth_found.after(b))
                for j in range(KT):
                    v.match_replace(rest[:, j, :], ninth[:, j, :], rest[:, j, :], GONE)\
                        .then_inc(ninth_gone.sem, 1)

            def a_softmax(b):
                dve.wait_ge(exp_out.sem, exp_out.after(b))
                for j in range(KT):
                    dve.wait_ge(ninth_gone.sem, ninth_gone.after(b, j + 1))
                    v.scalar_tensor_tensor(out=prob[:, j, :], in0=rest[:, j, :], scalar=GONE_MAX,
                                           in1=prob[:, j, :], op0=ALU.is_le, op1=ALU.mult,
                                           accum_out=psum_w[:, j:j + 1]).then_inc(prob_masked.sem, 1)
                dve.wait_ge(prob_masked.sem, prob_masked.after(b))
                v.reciprocal(rec_w[:, :], psum_w[:, :]).then_inc(rec_out.sem, 1)

            def a_products(b, n):
                if n == 0:
                    dve.wait_ge(mm_wre.sem, mm_wre.after(b))
                    dve.wait_ge(vagg_out.sem, vagg_out.after(b))
                if n == 2:
                    dve.wait_ge(mm_wim.sem, mm_wim.after(b))
                place = [agg_re, agg_im, v_im[:, :], v_re[:, :]][n]
                v.tensor_tensor(place, [pa_lo, pa_hi][n // 2], [v_re, v_im, v_im, v_re][n][:, :], ALU.mult)\
                    .then_inc(prod_w.sem, 1)

            def a_residual(b):
                dve.wait_ge(mm_agg.sem, mm_agg.after(b))
                dve.wait_ge(xres_in.sem, xres_in.after(b))
                if not first(b):
                    dve.wait_ge(x2_moved.sem, x2_moved.after(b - 1))
                v.tensor_tensor(x_b[:, :], pa_lo, x_res[:, :], ALU.add).then_inc(x1_out.sem, 1)

            def b_norm(b, n, before):
                dve.wait_ge(before.sem, before.after(b))
                layer_norm(b, n, x_b)

            def b_norm_rows(b, n):
                if n == 1:
                    if not first(b):
                        dve.wait_ge(mm_qq.sem, mm_qq.after(b - 1))
                else:
                    dve.wait_ge(tr_x[0].sem, tr_x[0].after(b))
                normalise(b, n, x_b, xn_b)

            def b_features(b, h):
                cols = slice(h * HALF, (h + 1) * HALF)
                dve.wait_ge(xt_out[0].sem, xt_out[0].after(b, h + 1))
                v.tensor_tensor(xt_l[:, cols], pb[:, h, :], xt_h[:, cols], ALU.subtract)\
                    .then_inc(xtl_out.sem, 1)

            def b_base(b):
                dve.wait_ge(mm_ffn[0].sem, mm_ffn[0].after(b))
                dve.wait_ge(bias_added.sem, bias_added.after(b))
                v.scalar_tensor_tensor(out=x_b[:, :], in0=pb_all, scalar=1.0 / W_SCALE, in1=x_b[:, :],
                                       op0=ALU.mult, op1=ALU.add).then_inc(x2_out.sem, 1)

            v_halves = words(v_pad[:, :])

            def low_half(place, column, high, signal):
                v.scalar_tensor_tensor(out=place, in0=pb_all, scalar=bias_att[:, column:column + 1], in1=high,
                                       op0=ALU.add, op1=ALU.subtract).then_inc(signal.sem, 1)

            def b_keys(b):
                dve.wait_ge(kh_out.sem, kh_out.after(b))
                low_half(k_l[:, PAD:PAD + D], 1, k_h[:, PAD:PAD + D], kl_out)

            def b_values_low(b):
                dve.wait_ge(vh_out.sem, vh_out.after(b))
                low_half(v_halves[:, PAD:PAD + D, LO], 2, v_halves[:, PAD:PAD + D, HI], vl_out)

            def b_values(b, odd):
                if odd == 0:
                    dve.wait_ge(vl_out.sem, vl_out.after(b))
                    dve.wait_ge(mm_ffn[0].sem, mm_ffn[0].after(b))
                elif not first(b):
                    dve.wait_ge(tr_x[1].sem, tr_x[1].after(b - 1))
                v.transpose(v_t[odd], v_pad[:, odd * QB:odd * QB + D]).then_inc(vt_out.sem, 1)

            def b_queries(b):
                dve.wait_ge(qh_out.sem, qh_out.after(b))
                low_half(words(q_hl)[:, :, LO], 0, words(q_hl)[:, :, HI], ql_out)

            def gates(b, n, source, experts, scale):
                g = gt[n]
                width = experts * RANK
                logit_scale = [1.0 / W_SCALE, 1.0][n]
                dve.wait_ge(mm_ra[n].sem, mm_ra[n].after(b))
                v.tensor_scalar(lg[n][:, 0:experts], source[:, 0, 0:experts], logit_scale, None, ALU.mult)\
                    .then_inc(g.sem, 1)
                dve_wait(dve, g, g.after(b, 1))
                v.max(lg_top[n][:, :], lg[n][:, 0:8]).then_inc(g.sem, 1)
                dve.wait_ge(g.sem, g.after(b, 2))
                v.tensor_copy(lg_pick[n][:, 0:2], lg_top[n][:, 0:2]).then_inc(g.sem, 1)
                dve_wait(dve, g, g.after(b, 3))
                v.match_replace(lg_mark[n][:, :], lg_pick[n][:, :], lg[n][:, :], TAKEN).then_inc(g.sem, 1)
                v.tensor_scalar(lg_neg[n][:, :], lg_top[n][:, 0:1], -1.0, None, ALU.mult).then_inc(g.sem, 1)
                dve.wait_ge(g.sem, g.after(b, 5))
                dve.wait_ge(gt_exp[n].sem, gt_exp[n].after(b))
                v.scalar_tensor_tensor(out=gate[n][:, 0:experts], in0=lg_mark[n][:, 0:experts],
                                       scalar=TAKEN_MIN, in1=lg_exp[n][:, 0:experts], op0=ALU.is_ge,
                                       op1=ALU.mult, accum_out=gate_sum[n][:, :]).then_inc(g.sem, 1)
                dve.wait_ge(g.sem, g.after(b, 6))
                v.reciprocal(gate_rec[n][:, :], gate_sum[n][:, :]).then_inc(g.sem, 1)
                dve.wait_ge(g.sem, g.after(b, 7))
                v.tensor_scalar(gate[n][:, 0:experts], gate[n][:, 0:experts], gate_rec[n][:, :], scale,
                                ALU.mult, ALU.mult).then_inc(g.sem, 1)
                dve.wait_ge(g.sem, g.after(b, 8))
                v.tensor_tensor(mid[n][:, :].rearrange("p (e r) -> p e r", r=RANK),
                                source[:, 0, experts:experts + width].rearrange("p (e r) -> p e r", r=RANK),
                                gate[n][:, 0:experts].unsqueeze(2).to_broadcast([P, experts, RANK]),
                                ALU.mult).then_inc(mid_out[n].sem, 1)

            def c_scores(b, g):
                source = pc[:, 0, :].rearrange("p (n k) -> p n k", k=KEYS)
                blocks = slice(g * GB, (g + 1) * GB)
                dve.wait_ge(mm_sc.sem, mm_sc.after(b, g + 1))
                v.tensor_reduce(sc_max[:, blocks], source, AX_X, ALU.max).then_inc(max_out.sem, 1)

            def c_subtract(b, g):
                source = pc[:, 0, :].rearrange("p (n k) -> p n k", k=KEYS)
                blocks = slice(g * GB, (g + 1) * GB)
                dve.wait_ge(max_out.sem, max_out.after(b, g + 1))
                v.tensor_tensor(sc[:, g % 2, :, :], source,
                                sc_max[:, blocks].unsqueeze(2).to_broadcast([P, GB, KEYS]),
                                ALU.subtract).then_inc(sc_in.sem, 1)

            def c_sums(b, g):
                blocks = slice(g * GB, (g + 1) * GB)
                dve.wait_ge(sc_exp.sem, sc_exp.after(b, g + 1))
                v.tensor_reduce(sc_sum[:, blocks], sc[:, g % 2, :, :], AX_X, ALU.add).then_inc(sum_out.sem, 1)
                dve.wait_ge(sum_out.sem, sum_out.after(b, g + 1))
                v.reciprocal(sc_rec[:, blocks], sc_sum[:, blocks]).then_inc(srec_out.sem, 1)

            def c_transpose(b, g):
                dve.wait_ge(pl_out.sem, pl_out.after(b, g + 1))
                if g >= 2:
                    dve.wait_ge(mm_av.sem, mm_av.after(b, g - 1))
                v.transpose(sc_t[:, g % 2, :, :].rearrange("p n k -> p (n k)"),
                            p_hl[:, g % 2, :, :].rearrange("p n k -> p (n k)")).then_inc(pt_out.sem, 1)

            def c_attention_residual(b):
                dve.wait_ge(mm_o.sem, mm_o.after(b))
                dve.wait_ge(x2_moved.sem, x2_moved.after(b))
                v.scalar_tensor_tensor(out=rows_c[:, :], in0=pc_all, scalar=bias_att[:, 3:4], in1=x_c[:, :],
                                       op0=ALU.add, op1=ALU.add).then_inc(x3_out.sem, 1)

            def c_norm(b):
                dve.wait_ge(x3_out.sem, x3_out.after(b))
                layer_norm(b, 3, rows_c)

            def c_norm_rows(b):
                normalise(b, 3, rows_c, xn_c)

            def c_result(b):
                dve.wait_ge(mm_ffn[1].sem, mm_ffn[1].after(b))
                v.tensor_tensor(rows_c[:, :], pc_all, rows_c[:, :], ALU.add).then_inc(x4_out.sem, 1)

            def step(i, do_a, do_b, do_c, do_next):
                b, c = i - 1, i - 2
                if do_b:
                    b_norm(b, 1, x1_out)
                    variance(b, 1)
                    for k in range(3):
                        root(b, 1, k)
                if do_c:
                    c_scores(c, 0)
                if do_b:
                    root(b, 1, 3)
                if do_c:
                    c_subtract(c, 0)
                if do_b:
                    for k in range(4, RSQRT_STEPS):
                        root(b, 1, k)
                    b_norm_rows(b, 1)
                if do_c:
                    c_scores(c, 1)
                    c_subtract(c, 1)
                    c_sums(c, 0)
                if do_b:
                    b_features(b, 0)
                    b_features(b, 1)
                if do_c:
                    c_sums(c, 1)
                    c_scores(c, 2)
                    c_transpose(c, 0)
                    c_subtract(c, 2)
                if do_b:
                    gates(b, 0, pb, E0, SCALE0)
                if do_c:
                    c_sums(c, 2)
                    c_scores(c, 3)
                if do_a:
                    a_product(i)
                if do_c:
                    c_transpose(c, 1)
                if do_next:
                    a_norm(i + 1)
                if do_c:
                    c_subtract(c, 3)
                    c_sums(c, 3)
                if do_next:
                    variance(i + 1, 0)
                if do_c:
                    c_transpose(c, 2)
                if do_a:
                    a_top(i, 0)
                    a_top(i, 1)
                if do_c:
                    c_transpose(c, 3)
                if do_a:
                    a_ninth(i)
                if do_next:
                    for k in range(2):
                        root(i + 1, 0, k)
                if do_a:
                    a_softmax(i)
                if do_b:
                    b_base(b)
                    b_norm(b, 2, x2_out)
                    variance(b, 2)
                    root(b, 2, 0)
                if do_next:
                    root(i + 1, 0, 2)
                if do_b:
                    for k in range(1, RSQRT_STEPS):
                        root(b, 2, k)
                if do_c:
                    c_attention_residual(c)
                    c_norm(c)
                    variance(c, 3)
                if do_next:
                    root(i + 1, 0, 3)
                if do_c:
                    for k in range(4):
                        root(c, 3, k)
                if do_b:
                    b_norm_rows(b, 2)
                    b_keys(b)
                if do_c:
                    root(c, 3, 4)
                if do_next:
                    root(i + 1, 0, 4)
                if do_c:
                    root(c, 3, 5)
                if do_a:
                    a_products(i, 0)
                if do_c:
                    root(c, 3, 6)
                if do_a:
                    a_products(i, 1)
                if do_c:
                    c_norm_rows(c)
                if do_b:
                    b_values_low(b)
                if do_a:
                    a_products(i, 2)
                if do_next:
                    root(i + 1, 0, 5)
                if do_a:
                    a_products(i, 3)
                if do_next:
                    root(i + 1, 0, 6)
                if do_b:
                    b_values(b, 0)
                    b_queries(b)
                if do_c:
                    gates(c, 1, pc, E1, SCALE1)
                if do_next:
                    a_norm_rows(i + 1)
                if do_b:
                    b_values(b, 1)
                if do_a:
                    a_residual(i)
                if do_c:
                    c_result(c)

            a_norm(0)
            variance(0, 0)
            for k in range(RSQRT_STEPS):
                root(0, 0, k)
            a_norm_rows(0)
            v.memset(ninth[:, :, :], GONE).then_inc(const_set.sem, 1)
            v.memset(one[:, :], 1.0).then_inc(const_set.sem, 1)
            v.memset(lg[0][:, :], GONE).then_inc(const_set.sem, 1)
            v.memset(lg[1][:, :], GONE).then_inc(const_set.sem, 1)
            v.memset(lg_pick[0][:, :], GONE).then_inc(const_set.sem, 1)
            v.memset(lg_pick[1][:, :], GONE).then_inc(const_set.sem, 1)
            v.memset(k_h[:, :], 0.0).then_inc(const_set.sem, 1)
            v.memset(k_l[:, :], 0.0).then_inc(const_set.sem, 1)
            v.memset(v_pad[:, :], 0.0).then_inc(const_set.sem, 1)
            dve.wait_ge(tab_in.sem, TABLES_IN)
            v.tensor_copy(ident_bf[:, :], ident[:, :])
            v.tensor_copy(band_bf[:, :], band_mask[:, :]).then_inc(const_set.sem, 1)
            dve.wait_ge(const_set.sem, CONSTS_SET)
            step(0, True, False, False, True)
            for n, (part, high, whole) in enumerate(((w_base_l, w_base_h, base_f32), (w_ra0_l, w_ra0_h, ra0_f32))):
                dve.wait_ge(w_hi.sem, n + 1)
                v.scalar_tensor_tensor(out=part[:, :, :].rearrange("p k n -> p (k n)"), in0=whole,
                                       scalar=W_SCALE, in1=high[:, :, :].rearrange("p k n -> p (k n)"),
                                       op0=ALU.mult, op1=ALU.subtract).then_inc(w_lo.sem, 1)
            dve.wait_ge(const_in.sem, CONSTS_IN)
            step(1, True, True, False, True)
            step(2, True, True, True, True)
            with dve.Fori(3, BATCH - 1) as i:
                step(i, True, True, True, True)
            step(BATCH - 1, True, True, True, False)
            step(BATCH, False, True, True, False)
            step(BATCH + 1, False, False, True, False)

        @block.gpsimd
        def _(pool):
            g_ = nc.gpsimd

            def b_bias(b):
                pool.wait_ge(ln_out[1].sem, ln_out[1].after(b))
                g_.tensor_tensor(x_b[:, :], x_b[:, :], bias_base[:, :], ALU.add).then_inc(bias_added.sem, 1)

            def b_move(b):
                pool.wait_ge(x2_out.sem, x2_out.after(b))
                if not first(b):
                    pool.wait_ge(x3_out.sem, x3_out.after(b - 1))
                g_.tensor_tensor(x_c[:, :], x_b[:, :], one[:, :].to_broadcast([P, D]), ALU.mult)\
                    .then_inc(x2_moved.sem, 1)

            def a_product(b):
                pool.wait_ge(q_out.sem, q_out.after(b))
                pool.wait_ge(v_out.sem, v_out.after(b))
                g_.tensor_tensor(c2, q_spec[:, :], v_im[:, :], ALU.mult).then_inc(prod_q2.sem, 1)

            def a_sum(b, n):
                pool.wait_ge(prod_w.sem, prod_w.after(b, n + 3))
                g_.tensor_tensor([agg_re, agg_im][n], [agg_re, agg_im][n], [v_im, v_re][n][:, :],
                                 [ALU.add, ALU.subtract][n]).then_inc(sum_w.sem, 1)

            def c_low(b, g):
                part = words(p_hl[:, g % 2, :, :])
                pool.wait_ge(ph_out.sem, ph_out.after(b, g + 1))
                g_.tensor_tensor(part[:, :, :, LO], sc[:, g % 2, :, :], part[:, :, :, HI], ALU.subtract)\
                    .then_inc(pl_out.sem, 1)

            def a_normalise(b):
                pool.wait_ge(rec_out.sem, rec_out.after(b))
                g_.tensor_tensor(prob[:, :, :], prob[:, :, :],
                                 rec_w[:, :].unsqueeze(2).to_broadcast([P, KT, P]), ALU.mult)\
                    .then_inc(prob_out.sem, 1)

            pool_rows = slice(32 * POOL_PAIR, 32 * POOL_PAIR + 32)

            def b_value_blocks(b, odd):
                pool.wait_ge(vt_out.sem, vt_out.after(b, odd + 1))
                if odd == 0:
                    if not first(b):
                        pool.wait_ge(mm_av.sem, mm_av.after(b - 1))
                else:
                    pool.wait_ge(vd_pool.sem, vd_pool.after(b, odd))
                place = v_diag[pool_rows, :, :, POOL_PAIR * HD:(POOL_PAIR + 1) * HD]\
                    .rearrange("p (m o) a d -> p o m a d", o=2)[:, odd]
                g_.tensor_tensor(place, v_t[odd][pool_rows, :].rearrange("p (m a d) -> p m a d", a=2, d=HD),
                                 one[pool_rows, :].unsqueeze(2).unsqueeze(3).to_broadcast([32, NBLK // 2, 2, HD]),
                                 ALU.mult).then_inc(vd_pool.sem, 1)

            def b_query_blocks(b, a):
                if a == 0:
                    pool.wait_ge(ql_out.sem, ql_out.after(b))
                    pool.wait_ge(x2_moved.sem, x2_moved.after(b))
                    if not first(b):
                        pool.wait_ge(mm_sc.sem, mm_sc.after(b - 1))
                else:
                    pool.wait_ge(qd_pool.sem, qd_pool.after(b, a))
                col = (2 * POOL_PAIR + a) * QB
                g_.tensor_tensor(q_diag[pool_rows, :, col:col + QB],
                                 q_hl[pool_rows, :].rearrange("p (n t) -> p n t", t=QB),
                                 par[pool_rows, a:a + 1].unsqueeze(2).to_broadcast([32, NBLK, QB]),
                                 ALU.mult).then_inc(qd_pool.sem, 1)

            def c_normalise(b, g):
                blocks = slice(g * GB, (g + 1) * GB)
                pool.wait_ge(srec_out.sem, srec_out.after(b, g + 1))
                g_.tensor_tensor(sc[:, g % 2, :, :], sc[:, g % 2, :, :],
                                 sc_rec[:, blocks].unsqueeze(2).to_broadcast([P, GB, KEYS]), ALU.mult)\
                    .then_inc(p_out.sem, 1)

            def step(i, do_a, do_b, do_c):
                b, c = i - 1, i - 2
                if do_c:
                    pool.wait_ge(vd_pool.sem, vd_pool.after(c))
                if do_c:
                    c_normalise(c, 0)
                    c_low(c, 0)
                    c_normalise(c, 1)
                if do_a:
                    a_product(i)
                if do_c:
                    c_low(c, 1)
                    c_normalise(c, 2)
                    c_low(c, 2)
                    c_normalise(c, 3)
                if do_b:
                    b_bias(b)
                if do_c:
                    c_low(c, 3)
                if do_a:
                    a_normalise(i)
                    a_sum(i, 0)
                    a_sum(i, 1)
                if do_b:
                    b_move(b)
                    b_query_blocks(b, 0)
                    b_query_blocks(b, 1)
                    b_value_blocks(b, 0)
                    b_value_blocks(b, 1)

            pool.wait_ge(tab_in.sem, TABLES_IN)
            pool.wait_ge(const_set.sem, CONSTS_SET)
            step(0, True, False, False)
            pool.wait_ge(w_lo.sem, WEIGHTS_SPLIT)
            g_.memset(v_diag[:, :, :, :], 0.0).then_inc(diag_set.sem, 1)
            g_.memset(q_diag[:, :, :], 0.0).then_inc(diag_set.sem, 1)
            pool.wait_ge(diag_set.sem, 2)
            step(1, True, True, False)
            step(2, True, True, True)
            with pool.Fori(3, BATCH) as i:
                step(i, True, True, True)
            step(BATCH, False, True, True)
            step(BATCH + 1, False, False, True)


_OUTS = [((32, 128, 1024), "float32")]


def kernel(**inputs):
    import concourse.bacc as bacc
    from concourse.bass_utils import run_bass_kernel_spmd as run

    f = {k: np.asarray(v) for k, v in inputs.items()}

    def tiles(w):
        return w.T.reshape(8, 128, -1).transpose(1, 0, 2)

    head_order = [2 * pair + a for a in range(2) for pair in range(4)]
    channels = np.concatenate([np.arange(16 * h, 16 * h + 16) for h in head_order])
    key = np.arange(32)[None, :] - (np.arange(128) % 16)[:, None]
    odd_head = (np.arange(128) // 16) % 2
    data = {
        "x": f["x"],
        "ctx_in": f["ctx_4096"],
        "spectra": spectral_tables(),
        "identity": np.eye(128, dtype=np.float32),
        "band": np.where((key >= 0) & (key < 16), 0.0, GONE).astype(np.float32),
        "parity": np.stack([1 - odd_head, odd_head], 1).astype(np.float32),
        "base_w": tiles(f["L0_ffn_W_base"]),
        "base_b": f["L0_ffn_b_base"],
        "ra0": tiles(np.concatenate([f["L0_ffn_W_router"], f["L0_ffn_A_stack"].reshape(128, 1024)])),
        "b0": f["L0_ffn_B_stack"].transpose(0, 2, 1).reshape(128, 1024),
        "wqkvo": np.stack([f["L1_xattn_Wq"].T, f["L1_xattn_Wk"].T, f["L1_xattn_Wv"].T,
                           f["L1_xattn_Wo"].T[channels]], 1),
        "biases": np.stack([f["L1_xattn_bq"], f["L1_xattn_bk"], f["L1_xattn_bv"], f["L1_xattn_bo"]], 1),
        "ra1": tiles(np.concatenate([f["L1_ffn_Wr"], f["L1_ffn_A"].reshape(64, 1024)])),
        "b1": f["L1_ffn_B"].transpose(0, 2, 1).reshape(64, 1024),
    }
    nc = bacc.Bacc("TRN2", target_bir_lowering=False, num_devices=1)
    arrays, args = {}, []
    for name, a in data.items():
        a = np.ascontiguousarray(a)
        arrays[f"in_{name}"] = a
        args.append(nc.dram_tensor(f"in_{name}", a.shape, mybir.dt.from_np(a.dtype), kind="ExternalInput").ap())
    shape, dtype = _OUTS[0]
    args.append(nc.dram_tensor("out_0", shape, mybir.dt.from_np(np.dtype(dtype)), kind="ExternalOutput").ap())
    build(nc, *args)
    r = run(nc, [arrays], core_ids=[0])
    return r.results[0]["out_0"]
```
